# Optimizing a Trainium2 kernel written in Bass

```python
import numpy as np
import jax
import jax.numpy as jnp

def _softmax(x, axis=-1):
    return jax.nn.softmax(x, axis=axis)

def _gelu(x):
    return jax.nn.gelu(x, approximate=True)

def _silu(x):
    return jax.nn.silu(x)

def _sigmoid(x):
    return jax.nn.sigmoid(x)

def _layernorm(x, axis=-1, eps=1e-05):
    m = jnp.mean(x, axis=axis, keepdims=True)
    v = jnp.var(x, axis=axis, keepdims=True)
    return (x - m) / jnp.sqrt(v + eps)

def _scatter_add(tgt, idx, src, axis=0):
    return tgt.at[idx].add(src)

def _segment_sum(src, seg, n):
    return jax.ops.segment_sum(src, seg, n)
kernel_name = 'mk_gps_d1_gnn_r8_c86d9b'

def setup_inputs(seed: int=0):
    np.random.seed(seed)
    _w = jnp.asarray

    def _rec_inputs():
        import jax
        import jax.numpy as jnp
        _gk = jax.random.key(seed)
        x = -6.415e-05 + 1 * jax.random.normal(jax.random.fold_in(_gk, 1), (1250, 1024), jnp.float32)
        _s = jax.random.randint(jax.random.fold_in(_gk, 2), (20000,), 0, 1250, jnp.int32)
        _d = jax.random.randint(jax.random.fold_in(_gk, 3), (20000,), 0, 1250, jnp.int32)
        _loop = jnp.arange(1250, dtype=jnp.int32)
        src = jnp.concatenate([_s, _d, _loop])
        dst = jnp.concatenate([_d, _s, _loop])
        _o = jnp.argsort(dst, stable=True)
        src = src[_o]
        dst = dst[_o]
        return (x, src, dst)
    x, src, dst = _rec_inputs()

    def _L0_gnn_setup():
        import jax, jax.numpy as jnp
        import numpy as np
        NEG_SLOPE = 0.1
        EPS = 1e-05
        key = jax.random.key(seed)
        k1, k2, k3, k4, k5 = jax.random.split(key, 5)
        N, E, DIN, DOUT = (1250, 20000, 1024, 1024)
        x = jax.random.normal(k1, (N, DIN), dtype=jnp.float32)
        W = jax.random.normal(k2, (DIN, DOUT), dtype=jnp.float32) * 0.02
        a = jax.random.normal(k3, (1, 2 * DOUT), dtype=jnp.float32) * 0.02
        src = jax.random.randint(k4, (E,), 0, N, dtype=jnp.int64)
        dst = jax.random.randint(k5, (E,), 0, N, dtype=jnp.int64)
        return {'x': x, 'W': W, 'a': a, 'src': src, 'dst': dst}
    _L0_gnn_all = _L0_gnn_setup()
    _L0_gnn_in = {k: v for k, v in _L0_gnn_all.items() if k in ('W', 'a')}
    del _L0_gnn_all

    def _L0_mix_setup():
        import jax, jax.numpy as jnp
        import numpy as np
        NUM_HEADS = 16
        key = jax.random.key(seed)
        k1, k2, k3 = jax.random.split(key, 3)
        B, N, C = (4, 512, 1024)
        x = jax.random.normal(k1, (B, N, C), dtype=jnp.float32)
        w_qkv = jax.random.normal(k2, (3 * C, C), dtype=jnp.float32) * C ** (-0.5)
        w_proj = jax.random.normal(k3, (C, C), dtype=jnp.float32) * C ** (-0.5)
        b_proj = jnp.zeros((C,), dtype=jnp.float32)
        return {'x': x, 'w_qkv': w_qkv, 'w_proj': w_proj, 'b_proj': b_proj}
    _L0_mix_all = _L0_mix_setup()
    _L0_mix_in = {k: v for k, v in _L0_mix_all.items() if k in ('w_qkv', 'w_proj', 'b_proj')}
    del _L0_mix_all

    def _L0_ffn_setup():
        import jax, jax.numpy as jnp
        import numpy as np
        E = 8
        K = 2
        key = jax.random.key(seed)
        ks = jax.random.split(key, 6)
        B, S, D, F = (4, 256, 1024, 512)
        s_d = 1.0 / np.sqrt(D).astype(np.float32)
        s_f = 1.0 / np.sqrt(F).astype(np.float32)
        return {'x': jax.random.normal(ks[0], (B, S, D), jnp.float32), 'ln_w': jnp.ones((D,), jnp.float32), 'Wg': jax.random.normal(ks[1], (D, E), jnp.float32) * s_d, 'bg': jnp.zeros((E,), jnp.float32), 'W1a': jax.random.normal(ks[2], (E, D, F), jnp.float32) * s_d, 'b1a': jnp.zeros((E, F), jnp.float32), 'W1b': jax.random.normal(ks[3], (E, D, F), jnp.float32) * s_d, 'b1b': jnp.zeros((E, F), jnp.float32), 'W2': jax.random.normal(ks[4], (E, F, D), jnp.float32) * s_f, 'b2': jnp.zeros((E, D), jnp.float32)}
    _L0_ffn_all = _L0_ffn_setup()
    _L0_ffn_in = {k: v for k, v in _L0_ffn_all.items() if k in ('ln_w', 'Wg', 'bg', 'W1a', 'b1a', 'W1b', 'b1b', 'W2', 'b2')}
    del _L0_ffn_all
    return {'x': x, 'src': src, 'dst': dst, 'L0_gnn_W': _L0_gnn_in['W'], 'L0_gnn_a': _L0_gnn_in['a'], 'L0_mix_w_qkv': _L0_mix_in['w_qkv'], 'L0_mix_w_proj': _L0_mix_in['w_proj'], 'L0_mix_b_proj': _L0_mix_in['b_proj'], 'L0_ffn_ln_w': _L0_ffn_in['ln_w'], 'L0_ffn_Wg': _L0_ffn_in['Wg'], 'L0_ffn_bg': _L0_ffn_in['bg'], 'L0_ffn_W1a': _L0_ffn_in['W1a'], 'L0_ffn_b1a': _L0_ffn_in['b1a'], 'L0_ffn_W1b': _L0_ffn_in['W1b'], 'L0_ffn_b1b': _L0_ffn_in['b1b'], 'L0_ffn_W2': _L0_ffn_in['W2'], 'L0_ffn_b2': _L0_ffn_in['b2']}

def reference(x, src, dst, L0_gnn_W, L0_gnn_a, L0_mix_w_qkv, L0_mix_w_proj, L0_mix_b_proj, L0_ffn_ln_w, L0_ffn_Wg, L0_ffn_bg, L0_ffn_W1a, L0_ffn_b1a, L0_ffn_W1b, L0_ffn_b1b, L0_ffn_W2, L0_ffn_b2):
    import jax
    import jax.numpy as jnp

    def _L0_gnn_ref(x, W, a, src, dst):
        import jax, jax.numpy as jnp
        import numpy as np
        NEG_SLOPE = 0.1
        EPS = 1e-05
        N = x.shape[0]
        d = W.shape[1]
        h = x @ W
        a_l, a_r = (a[0, :d], a[0, d:])
        al = h @ a_l
        ar = h @ a_r
        e = jnp.exp(-jax.nn.leaky_relu(al[src] + ar[dst], negative_slope=NEG_SLOPE))
        rowsum = jax.ops.segment_sum(e, src, num_segments=N)
        h_prime = jax.ops.segment_sum(e[:, None] * h[dst], src, num_segments=N)
        h_prime = h_prime / (rowsum[:, None] + EPS)
        return jax.nn.elu(h_prime)

    def _L0_mix_ref(x, w_qkv, w_proj, b_proj):
        import jax, jax.numpy as jnp
        import numpy as np
        NUM_HEADS = 16
        B, N, C = x.shape
        H = NUM_HEADS
        D = C // H
        qkv = jnp.einsum('bnc,oc->bno', x, w_qkv).reshape(B, N, 3, H, D)
        qkv = jnp.transpose(qkv, (2, 0, 3, 1, 4))
        q, k, v = (qkv[0], qkv[1], qkv[2])
        q = jax.nn.softmax(q, axis=-1)
        k = jax.nn.softmax(k, axis=-2)
        context = jnp.einsum('bhnd,bhne->bhde', k, v)
        attn = jnp.einsum('bhnd,bhde->bhne', q, context)
        attn = jnp.transpose(attn, (0, 2, 1, 3)).reshape(B, N, C)
        out = jnp.einsum('bnc,oc->bno', attn, w_proj) + b_proj
        return out

    def _L0_ffn_ref(x, ln_w, Wg, bg, W1a, b1a, W1b, b1b, W2, b2):
        import jax, jax.numpy as jnp
        import numpy as np
        E = 8
        K = 2
        B, S, D = x.shape
        eps = jnp.finfo(x.dtype).eps
        xn = x * jax.lax.rsqrt(jnp.mean(x * x, axis=-1, keepdims=True) + eps) * ln_w
        logits = xn @ Wg + bg
        vals, idx = jax.lax.top_k(logits, K)
        topk_w = jax.nn.softmax(vals, axis=-1)
        we = jnp.sum(jax.nn.one_hot(idx, E, dtype=x.dtype) * topk_w[..., None], axis=-2)
        T = B * S
        xf = xn.reshape(T, D)
        wef = we.reshape(T, E).T

        def step(acc, params):
            W1a_e, b1a_e, W1b_e, b1b_e, W2_e, b2_e, w_e = params
            a = xf @ W1a_e + b1a_e
            b = xf @ W1b_e + b1b_e
            y = jax.nn.silu(a) * b @ W2_e + b2_e
            return (acc + w_e[:, None] * y, None)
        out0 = jnp.zeros_like(xf)
        out, _ = jax.lax.scan(step, out0, (W1a, b1a, W1b, b1b, W2, b2, wef))
        return out.reshape(B, S, D)
    xn = _layernorm(x, axis=-1)
    x = x + _L0_gnn_ref(xn, L0_gnn_W, L0_gnn_a, src, dst) + _L0_mix_ref(xn[None], L0_mix_w_qkv, L0_mix_w_proj, L0_mix_b_proj)[0]
    x = x + _L0_ffn_ref(_layernorm(x, axis=-1)[None], L0_ffn_ln_w, L0_ffn_Wg, L0_ffn_bg, L0_ffn_W1a, L0_ffn_b1a, L0_ffn_W1b, L0_ffn_b1b, L0_ffn_W2, L0_ffn_b2)[0]
    return x

_drawn_inputs = setup_inputs


def setup_inputs(seed=0):
    import zlib

    import numpy as np

    out = dict(_drawn_inputs(seed))
    spreads = {'L0_mix_b_proj': (0.0, 0.1),
     'L0_ffn_ln_w': (1.0, 0.2),
     'L0_ffn_bg': (0.0, 0.1),
     'L0_ffn_b1a': (0.0, 0.1),
     'L0_ffn_b1b': (0.0, 0.1),
     'L0_ffn_b2': (0.0, 0.1)}
    factors = {}
    for name, (base, spread) in spreads.items():
        noise = np.random.default_rng([zlib.crc32(name.encode()), seed]).standard_normal(out[name].shape)
        drawn = base * np.exp(spread * noise) if base else spread * noise
        out[name] = jnp.asarray(drawn.astype(out[name].dtype))
    for name, factor in factors.items():
        out[name] = (out[name] * factor).astype(out[name].dtype)
    return out
```

```python
from contextlib import ExitStack

import concourse.bass as bass
from concourse import mybir

F32 = mybir.dt.float32
F16 = mybir.dt.float16
BF16 = mybir.dt.bfloat16
I32 = mybir.dt.int32
ALU = mybir.AluOpType
ACT = mybir.ActivationFunctionType
AX = mybir.AxisListType.X

P = 128
HALF = 512
UNIT = 4
MIN_STEPS = 2
SLOPE = 0.1
EPS_LN = 1e-5
EPS_GNN = 1e-5
EPS_RMS = 1.1920928955078125e-07
X_UP, W_UP = 2.0 ** 10, 2.0 ** 10
H_UP = 2.0 ** 6
K_UP = Q_UP = 2.0 ** 10
C_UP = 4.0
M_UP = 2.0 ** 12
F_UP = 2.0 ** 8
G_UP = 2.0 ** 4
BIG = 1024.0


def ds(start, size):
    return bass.ds(start, size)


def build(nc, x, src_t, dst_t, dst_rows, W, a, wqkv, wproj, bproj, ln_w, Wg, bg, W1a, b1a, W1b, b1b, W2, b2, out):
    N, D = out.shape
    NT = x.shape[0] // P
    NP = NT * P
    LAST = N - (NT - 1) * P
    KD = D // P
    ET = src_t.shape[1]
    EG = dst_rows.shape[1]
    ER = ET - (UNIT - 1)
    NE, _, F = W1a.shape
    KF = F // P
    NPAIR = D // P
    TOPK = 2
    SLOTS = (TOPK * N + NE * (P - 1)) // P
    assert NT == 10 and KD == 8 and F == HALF and D == 2 * HALF and SLOTS == 27 and ER <= HALF

    x1_dram = nc.dram_tensor("x1_scratch", (NP, D), F32, kind="Internal").ap()
    x2_dram = nc.dram_tensor("x2_scratch", (NP, D), F32, kind="Internal").ap()
    xf_dram = nc.dram_tensor("xf_scratch", (NP, D), F32, kind="Internal").ap()
    y_dram = nc.dram_tensor("y_scratch", (SLOTS * P, D), F32, kind="Internal").ap()

    with ExitStack() as ctx:
        def sb(name, shape, dt):
            return ctx.enter_context(nc.sbuf_tensor(name, shape, dt))

        def sem(name):
            return ctx.enter_context(nc.semaphore(name))

        ident = sb("ident", [P, P], F32)
        iota_n = sb("iota_n", [P, NP], F16)
        tri = sb("tri", [P, P], BF16)
        ones_b = sb("ones_b", [P, P], BF16)
        ones_f = sb("ones_f", [P, P], F32)
        ones_h = sb("ones_h", [P, 2], F16)
        zero_h = sb("zero_h", [P, HALF], F16)
        eps_ln = sb("eps_ln", [P, 1], F32)
        eps_rms = sb("eps_rms", [P, 1], F32)
        src_f = sb("src_f", [P, ET], F32)
        dst_f = sb("dst_f", [P, ET], F32)
        bproj_b = sb("bproj_b", [P, D], F32)
        lnw_b = sb("lnw_b", [P, D], F32)
        wg_sb = sb("wg_sb", [P, KD, NE], F32)
        bg_b = sb("bg_b", [P, NE], F32)
        stats = sb("stats", [P, 2, 12], F32)
        mv = sb("mv", [P, 2, 2], F32)
        sd = sb("sd", [P, 2, 1], F32)
        rstd = sb("rstd", [P, 2, 1], F32)
        nbias = sb("nbias", [P, 2, 1], F32)
        al_part = sb("al_part", [P, 2, 2, NT], F32)
        al_ar = sb("al_ar", [P, 2, NT], F32)
        ks = sb("ks", [P, KD], F32)
        rks = sb("rks", [P, KD], F32)
        kmax = sb("kmax", [P, 2, 2], F32)
        qred = sb("qred", [P, 2, 3, 8], F32)
        rsum = sb("rsum", [P, 2, 3], F32)
        urep = sb("urep", [P, 2, EG, 16], F32)
        ured = sb("ured", [P, 2, EG], F32)
        win = sb("win", [16, 8], F32)
        wini = sb("wini", [16, 2], I32)
        iota_w = sb("iota_w", [16, 2], F32)
        lohi = sb("lohi", [1, 32], I32)
        iota_e = sb("iota_e", [P, NE], F32)
        valid = sb("valid", [P, 1], F32)
        lg = sb("lg", [P, NE], F32)
        top8 = sb("top8", [P, 8], F32)
        idx8 = sb("idx8", [P, 8], mybir.dt.uint32)
        idxf = sb("idxf", [P, 8], F32)
        ssq = sb("ssq", [P, 3], F32)
        onehot = sb("onehot", [P, TOPK, NT, NE], F32)
        mask = sb("mask", [P, NT, NE], BF16)
        before = sb("before", [P, NT + 1, NE], BF16)
        wdiff = sb("wdiff", [P, NT], F32)
        wexp = sb("wexp", [P, NT], F32)
        wts = sb("wts", [P, TOPK, NT], F32)
        rank = sb("rank", [P, NT, NE], F32)
        ranked = sb("ranked", [P, NT, NE], F32)
        tot = sb("tot", [P, 6, NE], F32)
        toti = sb("toti", [P, 3, NE], I32)
        posf = sb("posf", [P, TOPK, NT], F32)
        pos = sb("pos", [P, TOPK, NT], I32)
        tok = sb("tok", [P, NT], F32)
        iota_s = sb("iota_s", [P, SLOTS + 1], F32)
        tile_i = sb("tile_i", [P, TOPK, NT], I32)
        tile_f = sb("tile_f", [P, TOPK, NT], F32)
        row_f = sb("row_f", [P, TOPK, NT], F32)
        slot_sb = sb("slot_sb", [P, SLOTS + 1], I32)

        base = (nc.sbuf_base + 63) // 64 * 64
        ctx.enter_context(nc.sbuf_tensor("arena", [P, (nc.sbuf_usable_end - 64 - base) // 64 * 16 - 32], F32))
        KB = 1024

        def at(name, kb, shape, dt):
            return nc.alloc_sbuf_tensor_at(name, shape, dt, offset=base + int(kb * KB))

        xt = [at(f"xt{p}", 20 * p, [P, KD, NP], F16) for p in range(2)]
        h = [at(f"h{p}", 40 + 20 * p, [P, NT, D], F16) for p in range(2)]
        adj = [at(f"adj{p}", 80 + 25.5 * p, [P, NT, NP], F16) for p in range(2)]
        w_sb = [[at(f"w{s}{p}", 132 + 16 * s + 8 * p, [P, KD, HALF], F16) for p in range(2)] for s in range(2)]
        stage = [at(f"stage{s}", 164 + 2 * s, [P, HALF], F32) for s in range(2)]
        stage_h = at("stage_h", 40, [P, KD, HALF], F32)
        x_in = [at(f"x_in{u}", 80 + 4 * u, [P, D], F32) for u in range(2)]
        x_n = [at(f"x_n{u}", 88 + 4 * u, [P, D], F32) for u in range(2)]
        a_b = at("a_b", 96, [P, 2, D], F32)
        junk = [at(f"junk{q}", 104 + 2 * q, [P, HALF], F32) for q in range(2)]
        idx_in = at("idx_in", 120, [P, 2, ET], I32)
        rows_i = at("rows_i", 108, [P, EG, P], I32)
        rows_f = at("rows_f", 110, [P, EG, P], F32)
        rtile = at("rtile", 112, [16, 4, ER], F32)
        iota_u = at("iota_u", 118, [16, ER], F32)
        oh_src = [at(f"oh_src{u}", 148 + 2.5 * u, [P, NP], F16) for u in range(UNIT)]
        al_rep = at("al_rep", 169, [P, NT, P], F32)
        al_row = at("al_row", 159, [P, NP], F32)
        edge = [at(f"edge{u}", 164 + 5 * u, [P, NP], F32) for u in range(2)]
        slope = at("slope", 174, [P, NP], F32)
        oh_dst = [at(f"oh_dst{u}", 179 + 0.25 * u, [P, P], F16) for u in range(UNIT)]
        x1 = [at(f"x1{u}", 168 + 4 * u, [P, D], F32) for u in range(2)]
        neg = at("neg", 176, [P, D], F32)
        poz = at("poz", 180, [P, D], F32)
        kv = [[at(f"kv{m}{p}", 40 + 20 * m + 10 * p, [P, NT, HALF], F16) for p in range(2)] for m in range(2)]
        k_exp = [at(f"k_exp{u}", 80 + 5 * u, [P, NP], F32) for u in range(2)]
        ctxt = [at(f"ctxt{p}", 90 + 2 * p, [P, NPAIR, P], F16) for p in range(2)]
        qt = [at(f"qt{p}", 40 + 20 * p, [P, KD, NP], F16) for p in range(2)]
        q_s = [at(f"q_s{u}", 168 + 2 * u, [P, HALF], F32) for u in range(2)]
        w_proj = [w_sb[0], [at(f"w_proj{p}", (172, 80)[p], [P, KD, HALF], F16) for p in range(2)]]
        m_sb = [at(f"m{p}", 94 + 16 * p, [P, KD, D], F16) for p in range(2)]
        x1m = [at(f"x1m{u}", 4 * u, [P, D], F32) for u in range(2)]
        x2m = [at(f"x2m{u}", 8 + 4 * u, [P, D], F32) for u in range(2)]
        xfm = [at(f"xfm{u}", 16 + 4 * u, [P, D], F32) for u in range(2)]
        oh_row = at("oh_row", 88, [P, TOPK * NT, P], F16)
        oh_tile = at("oh_tile", 126, [P, TOPK * NT, SLOTS + 1], F16)
        xft = at("xft", 24, [P, KD, P], F32)
        sqj = at("sqj", 28, [P, D], F32)
        ew = [[at(f"ew{s}{p}", (136, 88)[s] + 24 * p, [P, KD + KF, D], F16) for p in range(2)] for s in range(2)]
        est = [at(f"est{s}", (80, 84, 32, 36)[s], [P, D], F32) for s in range(4)]
        xg = at("xg", 0, [P, D], F32)
        xgt = [at(f"xgt{p}", 4 + 2 * p, [P, KD, P], F16) for p in range(2)]
        ga = at("ga", 8, [P, HALF], F32)
        gb = at("gb", 10, [P, HALF], F32)
        hid = at("hid", 12, [P, HALF], F32)
        hidt = [at(f"hidt{p}", 14 + p, [P, KF, P], F16) for p in range(2)]
        y_sb = at("y_sb", 16, [P, D], F32)
        eb = [at(f"eb{s}", 20 + 20 * s, [P, 2 * D], F32) for s in range(2)]
        RING = 8
        yg = [at(f"yg{q}", 48 + 4 * q, [P, D], F32) for q in range(RING)]
        x2e = at("x2e", 136, [P, NT, D], F32)

        ps = ctx.enter_context(nc.psum_tensor("ps", [P, 8, HALF], F32))

        def banks(b, n):
            return ps[:, b:b + n, :].rearrange("p b n -> p (b n)")

        const_set = sem("const_set"); const_ld = sem("const_ld"); dve_c = sem("dve_c")
        idx_ready = sem("idx_ready"); win_mm = sem("win_mm"); win_ready = sem("win_ready")
        stage_ld = [sem(f"stage_ld{s}") for s in range(2)]; wh_ld = [sem(f"wh_ld{g}") for g in range(KD // 2)]
        w_hi = sem("w_hi"); w_done = sem("w_done");
        xin_ld = [sem(f"xin_ld{u}") for u in range(2)]
        ln_mv = sem("ln_mv"); ln_sd = sem("ln_sd"); ln_nb = sem("ln_nb"); xn_ready = sem("xn_ready")
        xn_turned = sem("xn_turned"); xt_hi = sem("xt_hi"); xt_done = sem("xt_done")
        g_done = sem("g_done"); g_hi = sem("g_hi"); g_free = sem("g_free")
        dve_ln = sem("dve_ln")
        alrep_ready = sem("alrep_ready"); alrow_mm = sem("alrow_mm"); alrow_ready = sem("alrow_ready")
        oh_ready = sem("oh_ready");  oh_free = sem("oh_free"); win_done = sem("win_done")
        z_ready = sem("z_ready"); lr_ready = sem("lr_ready"); e_ready = sem("e_ready")
        cnt_ready = sem("cnt_ready"); adj_hi = sem("adj_hi"); adj_done = sem("adj_done")
        gnn_done = sem("gnn_done"); gnn_free = sem("gnn_free"); neg_ready = sem("neg_ready"); neg_exp = sem("neg_exp")
        dve_g = sem("dve_g"); x1_ready = sem("x1_ready")
        x1_ld = [sem(f"x1_ld{u}") for u in range(2)]; x1_st = [sem(f"x1_st{u}") for u in range(2)]
        k_done = sem("k_done"); km_ready = sem("km_ready"); ke_ready = sem("ke_ready"); dve_k = sem("dve_k")
        kt_mm = sem("kt_mm"); kt_hi = sem("kt_hi"); kt_done = sem("kt_done"); ke_zero = sem("ke_zero")
        ctx_mm = sem("ctx_mm"); ctx_hi = sem("ctx_hi"); ctx_done = sem("ctx_done")
        q_exp = sem("q_exp"); q_norm = sem("q_norm"); q_mm = sem("q_mm"); q_hi = sem("q_hi"); qt_done = sem("qt_done")
        dve_q = sem("dve_q")
        rks_ready = sem("rks_ready"); m_mm = sem("m_mm"); m_hi = sem("m_hi"); m_done = sem("m_done")
        mix_done = sem("mix_done"); x2_ready = sem("x2_ready"); ln2_mv = sem("ln2_mv"); ln2_sd = sem("ln2_sd"); ln2_nb = sem("ln2_nb")
        xn2_ready = sem("xn2_ready"); act_m = sem("act_m"); rms_sd = sem("rms_sd"); xf_ready = sem("xf_ready"); xf_mm = sem("xf_mm"); xft_ready = sem("xft_ready")
        lg_mm = sem("lg_mm"); lg_ready = sem("lg_ready"); dve_m = sem("dve_m"); dve_x = sem("dve_x"); wd_ready = sem("wd_ready"); we_ready = sem("we_ready")
        x1m_ld = [sem(f"x1m_ld{u}") for u in range(2)]; x2_st = [sem(f"x2_st{u}") for u in range(2)]; xf_st = [sem(f"xf_st{u}") for u in range(2)]
        mask_ready = sem("mask_ready"); rank_mm = sem("rank_mm"); dve_r = sem("dve_r"); pos_ready = sem("pos_ready")
        place_ready = sem("place_ready"); place_mm = sem("place_mm"); slots_ready = sem("slots_ready")
        est_ld = [sem(f"est_ld{s}") for s in range(4)]
        ew_hi = sem("ew_hi"); ew_done = sem("ew_done"); eb_ld = [sem(f"eb_ld{s}") for s in range(2)]
        xg_ld = sem("xg_ld"); xg_mm = sem("xg_mm"); xgt_hi = sem("xgt_hi"); xgt_done = sem("xgt_done")
        g1_done = sem("g1_done"); ab_done = sem("ab_done"); silu_done = sem("silu_done"); hid_ready = sem("hid_ready")
        hid_mm = sem("hid_mm"); hidt_hi = sem("hidt_hi"); hidt_done = sem("hidt_done"); g2_done = sem("g2_done"); y_ready = sem("y_ready"); y_st = sem("y_st"); y_fill = sem("y_fill")
        yg_ld = [sem(f"yg_ld{q}") for q in range(RING)]; x2e_ld = sem("x2e_ld")
        y_added = sem("y_added"); o_st = sem("o_st")

        halves = [W[:, 0:HALF], W[:, HALF:D]]
        for i in range(2):
            halves.append(wqkv[:, D + i * HALF:D + (i + 1) * HALF])
            halves.append(wqkv[:, 2 * D + i * HALF:2 * D + (i + 1) * HALF])
        halves += [wqkv[:, i * HALF:(i + 1) * HALF] for i in range(2)]
        J_K, J_V, J_Q, J_P = (2, 4), (3, 5), 6, 8
        BANK = {0: 4, 1: 4, 3: 0, 5: 3, 6: 3, 7: 3}
        G_BASE = {0: 0, 1: 10, 3: 20, 5: 30, 6: 40, 7: 50}

        def tiles(e, body, peel=1):
            body(0, 0, None, 0)
            with e.Fori(0, (NT - 1 - peel) // 2) as i:
                body(2 * i + 1, 1, i, 0)
                body(2 * i + 2, 0, i, 1)
            for t in range(NT - peel, NT - 1):
                body(t, t % 2, (t - 1) // 2, (t - 1) % 2)
            body(NT - 1, 1, None, 0)

        def turns(t, u, i, s):
            return (t // 2 + 1) if isinstance(t, int) else (i + 1 if s == 0 else i + 2)

        def split_mm(pe, outs, lhs, rhs, first, last, done=None):
            mm = None
            for n, o in enumerate(outs):
                pe.matmul(o, lhs[0], rhs[n][0], start=first, stop=False, skip_group_check=True)
                pe.matmul(o, lhs[0], rhs[n][1], start=False, stop=False, skip_group_check=True)
            for n, o in enumerate(outs):
                mm = pe.matmul(o, lhs[1], rhs[n][0], start=False, stop=last, skip_group_check=True)
            return mm

        def conv_act(act, j, i, u):
            act.wait_ge(stage_ld[u], 16 * (KD // 2 * (j - 1) + i + 1))
            if j - 2 in J_K:
                act.wait_ge(k_done, 4 * J_K.index(j - 2) + 4)
            elif j >= 2:
                act.wait_ge(g_done, G_BASE[j - 2] + NT)
            act.activation(w_sb[j % 2][0][:, ds(2 * i + u, 1), :], stage[u][:, :], ACT.Copy, scale=W_UP).then_inc(w_hi, 1)

        def conv_dve(dve, j, i, u):
            dve.wait_ge(w_hi, KD * j + 2 * i + u + 1)
            dve.scalar_tensor_tensor(w_sb[j % 2][1][:, ds(2 * i + u, 1), :], stage[u][:, :], W_UP,
                                     w_sb[j % 2][0][:, ds(2 * i + u, 1), :], ALU.mult, ALU.subtract).then_inc(w_done, 1)

        def pconv_act(act, c, u):
            act.wait_ge(stage_ld[u], 16 * (KD // 2 * (J_P - 1) + c + 1))
            act.wait_ge(g_done, G_BASE[J_Q] + NT)
            act.activation(w_proj[u][0][:, ds(c, 1), :], stage[u][:, :], ACT.Copy, scale=W_UP).then_inc(w_hi, 1)

        def pconv_dve(dve, c, u):
            dve.wait_ge(w_hi, KD * J_P + 2 * c + u + 1)
            dve.scalar_tensor_tensor(w_proj[u][1][:, ds(c, 1), :], stage[u][:, :], W_UP, w_proj[u][0][:, ds(c, 1), :],
                                     ALU.mult, ALU.subtract).then_inc(w_done, 1)

        def fconv_act(act, i, s):
            act.wait_ge(est_ld[s], 32 * (i + 1))
            act.activation(ew[0][0][:, ds(2 * i + s, 1), :], est[s][:, :], ACT.Copy, scale=W_UP).then_inc(ew_hi, 1)

        def fconv_dve(dve, i, s):
            dve.wait_ge(ew_hi, 2 * i + s + 1)
            dve.scalar_tensor_tensor(ew[0][1][:, ds(2 * i + s, 1), :], est[s][:, :], W_UP, ew[0][0][:, ds(2 * i + s, 1), :],
                                     ALU.mult, ALU.subtract).then_inc(ew_done, 1)

        def econv_act(act, e, slot, c, s):
            act.wait_ge(est_ld[s], 32 * (NC // 4 * e + c // 4 + (1 if s < 2 else 1 - KD // 4) + (KD // 4 if s < 2 else 0)))
            act.activation(ew[slot][0][:, c, :], est[s][:, :], ACT.Copy, scale=W_UP).then_inc(ew_hi, 1)

        def econv_dve(dve, e, slot, c, s):
            dve.wait_ge(ew_hi, (KD + KF) * e + c + 1)
            dve.scalar_tensor_tensor(ew[slot][1][:, c, :], est[s][:, :], W_UP, ew[slot][0][:, c, :],
                                     ALU.mult, ALU.subtract).then_inc(ew_done, 1)

        NC = KD + KF

        def wait_alone(e, s, value):
            value = value if isinstance(value, int) else e.to_reg(value)
            e.wait_ge(const_set, 19)
            e.wait_ge(s, value)

        block = ctx.enter_context(nc.Block())

        @block.sync
        def _(sp):
            sp.dma_start(x_in[0][:, :], x[0:P, :]).then_inc(xin_ld[0], 16)
            for g in range(KD // 2):
                sp.dma_start(stage_h[:, 2 * g:2 * g + 2, :],
                             halves[0][2 * g * P:(2 * g + 2) * P, :].rearrange("(k p) n -> p k n", p=P)).then_inc(wh_ld[g], 16)
                if g == 1:
                    sp.dma_start(x_in[1][:, :], x[P:2 * P, :]).then_inc(xin_ld[1], 16)
            for t_, s_ in ((a_b[:, 0, :], a[0:1, :].to_broadcast([P, D])), (a_b[:, 1, :], a[1:2, :].to_broadcast([P, D])),
                           (idx_in[:, 0, :], src_t), (idx_in[:, 1, :], dst_t), (rows_i[:, :, :], dst_rows),
                           (bproj_b[:, :], bproj.to_broadcast([P, D])), (lnw_b[:, :], ln_w.to_broadcast([P, D])),
                           (wg_sb[:, :, :], Wg.rearrange("(k p) e -> p k e", p=P)), (bg_b[:, :], bg.to_broadcast([P, NE]))):
                sp.dma_start(t_, s_).then_inc(const_ld, 16)
            sp.sem_inc(w_done, 2)

            def load_chunk(j, i, u):
                sp.wait_ge(w_done, KD * j + 2 * i + u + 1)
                sp.dma_start(stage[u][:, :], halves[j][ds((2 * i + u) * P, P), :]).then_inc(stage_ld[u], 16)

            def load_half(j):
                with sp.Fori(0, KD // 2) as i:
                    for u in range(2):
                        load_chunk(j, i, u)

            with sp.Fori(0, KD // 2) as i:
                for u in range(2):
                    sp.wait_ge(xn_ready, 2 * i + u + 1)
                    sp.dma_start(x_in[u][:, :], x[ds((2 * i + u + 2) * P, P), :]).then_inc(xin_ld[u], 16)
                    load_chunk(1, i, u)
            load_half(2)
            for u in range(2):
                if u == 0:
                    sp.wait_ge(adj_done, NT + 2)
                sp.dma_start(x1[u][:, :], x[u * P:(u + 1) * P, :]).then_inc(x1_ld[u], 16)

            def gnn_io(t, u, n, load):
                sp.wait_ge(x1_ready, t + 1)
                sp.dma_start(x1_dram[ds(t * P, P), :], x1[u][:, :]).then_inc(x1_st[u], 16)
                if load:
                    sp.wait_ge(x1_st[u], 16 * n)
                    sp.dma_start(x1[u][:, :], x[ds((t + 2) * P, P), :]).then_inc(x1_ld[u], 16)

            with sp.Fori(0, NT // 2 - 1) as i:
                for u in range(2):
                    gnn_io(2 * i + u, u, i + 1, True)
            for u in range(2):
                gnn_io(NT - 2 + u, u, NT // 2, False)
            for j in range(3, J_P):
                load_half(j)
            with sp.Fori(0, KD) as c:
                for u in range(2):
                    sp.wait_ge(w_done, KD * J_P + 2 * c + u + 1)
                    sp.dma_start(stage[u][:, :], wproj[ds(c * P, P), u * HALF:(u + 1) * HALF]).then_inc(stage_ld[u], 16)

            sp.sem_inc(ew_done, 4)
            for u in range(2):
                sp.sem_inc(x2_st[u], 16)
                sp.sem_inc(xf_st[u], 16)
            sp.sem_inc(y_st, 16)

            def load_expert(e, slot, bias_wait):
                for c in range(NC):
                    s = c % 4
                    sp.wait_ge(ew_done, NC * e + c + 1)
                    if c < KD:
                        sp.dma_start(est[s][:, 0:HALF], W1a[ds(e, 1), c * P:(c + 1) * P, :]).then_inc(est_ld[s], 16)
                        sp.dma_start(est[s][:, HALF:D], W1b[ds(e, 1), c * P:(c + 1) * P, :]).then_inc(est_ld[s], 16)
                    else:
                        sp.dma_start(est[s][:, :], W2[ds(e, 1), (c - KD) * P:(c - KD + 1) * P, :]).then_inc(est_ld[s], 32)
                if bias_wait:
                    sp.wait_ge(ew_done, 4 + NC * e + KD + 1)
                sp.dma_start(eb[slot][:, 0:F], b1a[ds(e, 1), :].to_broadcast([P, F])).then_inc(eb_ld[slot], 16)
                sp.dma_start(eb[slot][:, F:2 * F], b1b[ds(e, 1), :].to_broadcast([P, F])).then_inc(eb_ld[slot], 16)
                sp.dma_start(eb[slot][:, 2 * F:], b2[ds(e, 1), :].to_broadcast([P, D])).then_inc(eb_ld[slot], 16)

            def mix_io(t, u, n, load):
                if load:
                    sp.wait_ge(x2_ready, t + 3)
                    sp.dma_start(x1m[u][:, :], x1_dram[ds((t + 2) * P, P), :]).then_inc(x1m_ld[u], 16)
                else:
                    sp.wait_ge(x2_ready, t + 3)
                sp.dma_start(x2_dram[ds(t * P, P), :], x2m[u][:, :]).then_inc(x2_st[u], 16)
                sp.wait_ge(xf_ready, t + 1)
                sp.dma_start(xf_dram[ds(t * P, P), :], xfm[u][:, :]).then_inc(xf_st[u], 16)

            sp.wait_ge(qt_done, 2 * NT + 2)
            for u in range(2):
                sp.wait_ge(x1_st[u], 16 * NT // 2)
            for u in range(2):
                sp.dma_start(x1m[u][:, :], x1_dram[u * P:(u + 1) * P, :]).then_inc(x1m_ld[u], 16)
            def load_first(c, s):
                sp.wait_ge(ew_done, c + 3)
                sp.dma_start(est[s][:, 0:HALF], W1a[0:1, ds(c * P, P), :]).then_inc(est_ld[s], 16)
                sp.dma_start(est[s][:, HALF:D], W1b[0:1, ds(c * P, P), :]).then_inc(est_ld[s], 16)

            sp.wait_ge(m_done, 2 * KD + 2)
            with sp.Fori(0, NT // 2 - 1) as i:
                for u in range(2):
                    load_first(2 * i + u, u)
                    mix_io(2 * i + u, u, i + 1, True)
            for u in range(2):
                mix_io(NT - 2 + u, u, NT // 2, False)
            for c in range(KD, NC):
                sp.wait_ge(ew_done, c + 3)
                sp.dma_start(est[c % 4][:, :], W2[0:1, (c - KD) * P:(c - KD + 1) * P, :]).then_inc(est_ld[c % 4], 32)
            for u in range(2):
                sp.wait_ge(x2_st[u], 16 * (NT // 2 + 1))
                sp.wait_ge(xf_st[u], 16 * (NT // 2 + 1))
            sp.wait_ge(lg_ready, NT)
            sp.dma_start(eb[0][:, 0:F], b1a[0:1, :].to_broadcast([P, F])).then_inc(eb_ld[0], 16)
            sp.dma_start(eb[0][:, F:2 * F], b1b[0:1, :].to_broadcast([P, F])).then_inc(eb_ld[0], 16)
            sp.dma_start(eb[0][:, 2 * F:], b2[0:1, :].to_broadcast([P, D])).then_inc(eb_ld[0], 16)
            load_expert(1, 1, False)
            with sp.Fori(1, NE // 2) as j:
                load_expert(2 * j, 0, True)
                load_expert(2 * j + 1, 1, True)
            before_last = sp.value_load(toti[0:1, 2, NE - 2:NE - 1], min_val=NE - 1, max_val=SLOTS - 1)
            wait_alone(sp, g2_done, before_last)
            sp.dma_start(x2e[:, :, :], x2_dram.rearrange("(t p) d -> p t d", p=P)).then_inc(x2e_ld, 16)
            with sp.Fori(0, NT - 1) as t:
                sp.wait_ge(y_added, 2 * t + 2)
                sp.dma_start(out[ds(t * P, P), :], x2e[:, ds(t, 1), :]).then_inc(o_st, 16)
            sp.wait_ge(y_added, 2 * NT)
            sp.dma_start(out[(NT - 1) * P:N, :], x2e[0:LAST, NT - 1, :]).then_inc(o_st, 16)
            sp.wait_ge(o_st, 16 * NT)

        @block.gpsimd
        def _(pool):
            pool.memset(ident[:, :], 0.0).then_inc(const_set, 1)
            pool.memset(tri[:, :], 0.0).then_inc(const_set, 1)
            pool.memset(valid[:, :], 1.0).then_inc(const_set, 1)
            pool.wait_ge(const_set, 3)
            pool.affine_select(out=ident[:, :], in_=ident[:, :], compare_op=ALU.not_equal, fill=1.0, base=0,
                               pattern=[[-1, P]], channel_multiplier=1).then_inc(const_set, 1)
            pool.affine_select(out=tri[:, :], in_=tri[:, :], compare_op=ALU.is_ge, fill=1.0, base=0,
                               pattern=[[-1, P]], channel_multiplier=1).then_inc(const_set, 1)
            pool.affine_select(out=valid[:, :], in_=valid[:, :], compare_op=ALU.is_ge, fill=0.0, base=LAST - 1,
                               pattern=[[0, 1]], channel_multiplier=-1).then_inc(const_set, 1)
            for t_, pattern, b_, mult in ((iota_n, [[1, NP]], 0, 0), (iota_w, [[P, 2]], 0, P), (iota_u, [[1, ER]], 0, 0),
                                          (iota_e, [[1, NE]], 0, 0), (tok, [[P, NT]], 0, 1),
                                          (iota_s, [[1, SLOTS + 1]], 0, 0)):
                pool.iota(t_[:, :], pattern, base=b_, channel_multiplier=mult,
                          allow_small_or_imprecise_dtypes=True).then_inc(const_set, 1)
            pool.memset(ones_b[:, :], 1.0).then_inc(const_set, 1)
            pool.memset(ones_f[:, :], 1.0).then_inc(const_set, 1)
            pool.memset(ones_h[:, :], 1.0).then_inc(const_set, 1)
            pool.memset(zero_h[:, :], 0.0).then_inc(const_set, 1)
            pool.memset(eps_ln[:, :], EPS_LN).then_inc(const_set, 1)
            pool.memset(eps_rms[:, :], EPS_RMS).then_inc(const_set, 1)
            pool.memset(before[:, 0, :], 0.0).then_inc(const_set, 1)
            def window_pool(w, wu, i, s_):
                pool.wait_ge(z_ready, 3 * w + 3)
                pool.tensor_tensor(edge[wu][:, :], edge[wu][:, :], slope[:, :], ALU.add).then_inc(lr_ready, 1)

            tiles(pool, window_pool)
            pool.wait_ge(adj_done, NT + 2)
            pool.wait_ge(x1_ready, NT)
            for u in range(2):
                pool.memset(k_exp[u][:, N:NP], 0.0).then_inc(ke_zero, 1)
            for p_ in range(2):
                pool.memset(ctxt[p_][:, :, :], 0.0).then_inc(ke_zero, 1)

            pool.wait_ge(slots_ready, 1)
            for u in range(2):
                pool.wait_ge(xf_st[u], 16 * (NT // 2 + 1))
                pool.wait_ge(x2_st[u], 16 * (NT // 2 + 1))
            used = pool.value_load(toti[0:1, 2, NE - 1:NE], min_val=NE, max_val=SLOTS)

            def gather(s):
                if s:
                    pool.wait_ge(xg_mm, 2 * s)
                pool.indirect_dma_start(out=xg[:, :], out_offset=None, in_=xf_dram,
                                        in_offset=bass.IndirectOffsetOnAxis(ap=slot_sb[:, s:s + 1], axis=0)).then_inc(xg_ld, 16)

            for s in range(SLOTS + 1):
                if s <= NE:
                    gather(s)
                else:
                    with pool.If(used >= s):
                        gather(s)
            zeros = zero_h[:, :].bitcast(F32)
            fills = pool.alloc_register("pool_fills")
            pool.reg_mov(fills, 1)
            with pool.If(used < SLOTS):
                with pool.Fori(used, SLOTS) as s:
                    pool.dma_start(y_dram[ds(s * P, P), :].rearrange("p (r n) -> p r n", n=HALF // 2),
                                   zeros.unsqueeze(1).to_broadcast([P, 2 * D // HALF, HALF // 2])).then_inc(y_fill, 16)
                    pool.wait_ge(y_fill, 16 * pool.snap(fills, min_val=1, max_val=SLOTS))
                    pool.reg_add(fills, fills, 1)
            wait_alone(pool, y_st, 16 * used + 16)
            for q in range(TOPK * NT):
                t, k = q // TOPK, q % TOPK
                rows = LAST if t == NT - 1 else P
                if q >= RING:
                    pool.wait_ge(y_added, q - RING + 1)
                pool.indirect_dma_start(out=yg[q % RING][0:rows, :], out_offset=None, in_=y_dram,
                                        in_offset=bass.IndirectOffsetOnAxis(ap=pos[0:rows, k, t:t + 1], axis=0)).then_inc(yg_ld[q % RING], 16)

        @block.scalar
        def _(act):
            act.wait_ge(const_set, 19)
            act.sem_inc(xn_turned, 4)
            act.sem_inc(xf_mm, 4)

            def ln_norm(t, u):
                act.wait_ge(ln_mv, t + 1)
                act.activation(sd[:, u, :], mv[:, u, 1:2], ACT.Sqrt, bias=eps_ln[:, 0:1]).then_inc(ln_sd, 1)
                act.wait_ge(ln_nb, t + 1)
                act.wait_ge(xn_turned, 2 * t + 2)
                act.activation(x_n[u][:, :], x_in[u][:, :], ACT.Identity, bias=nbias[:, u, :], scale=rstd[:, u, :]).then_inc(xn_ready, 1)

            def xt_high(t, u):
                for b in range(2):
                    act.wait_ge(xn_turned, 2 * t + b + 5)
                    act.activation(xt[0][:, 4 * b:4 * b + 4, ds(t * P, P)], ps[:, 2 * u + b, :].rearrange("p (k n) -> p k n", k=4),
                                   ACT.Copy, scale=X_UP).then_inc(xt_hi, 1)

            def h_high(half):
                def body(t, u, i, s):
                    if half == 0 and not (isinstance(t, int) and t > NT - 2):
                        xt_high(t + 1, 1 - u)
                    if half == 0 and not (isinstance(t, int) and t > NT - 3):
                        ln_norm(t + 2, u)
                    if i is not None:
                        conv_act(act, half + 1, i, s)
                    act.wait_ge(g_done, G_BASE[half] + t + 1)
                    act.activation(h[0][:, ds(t, 1), half * HALF:(half + 1) * HALF], ps[:, 4 + u, :], ACT.Copy,
                                   scale=H_UP / (X_UP * W_UP)).then_inc(g_hi, 1)
                return body

            ln_norm(0, 0)
            for g in range(KD // 2):
                act.wait_ge(wh_ld[g], 16)
                act.activation(w_sb[0][0][:, 2 * g:2 * g + 2, :], stage_h[:, 2 * g:2 * g + 2, :], ACT.Copy, scale=W_UP).then_inc(w_hi, 2)
                if g == 1:
                    xt_high(0, 0)
                    ln_norm(1, 1)
            tiles(act, h_high(0), 3)
            tiles(act, h_high(1))
            for b, n in ((0, HALF), (1, HALF), (2, NP - 2 * HALF)):
                act.wait_ge(alrow_mm, 1)
                ins = act.activation(al_row[:, b * HALF:b * HALF + n], ps[:, b, 0:n], ACT.Copy)
            ins.then_inc(alrow_ready, 1)
            act.wait_ge(alrow_ready, 1)

            def window_act(w, wu, i, s_):
                act.wait_ge(adj_done, w + 1)
                act.activation(edge[wu][:, :], al_row[:, :], ACT.Identity, bias=al_ar[:, 1, ds(w, 1)]).then_inc(z_ready, 1)
                act.wait_ge(z_ready, 3 * w + 1)
                act.activation(slope[:, :], edge[wu][:, :], ACT.Relu, scale=1.0 - SLOPE).then_inc(z_ready, 1)
                act.activation(edge[wu][:, :], edge[wu][:, :], ACT.Copy, scale=SLOPE).then_inc(z_ready, 1)
                act.wait_ge(lr_ready, w + 1)
                act.activation(edge[wu][:, :], edge[wu][:, :], ACT.Exp, scale=-1.0).then_inc(e_ready, 1)
                if not (isinstance(w, int) and w == 0):
                    adj_high(w - 1, 1 - wu)

            def adj_high(w, wu):
                act.wait_ge(cnt_ready, w + 3)
                act.activation(adj[0][:, ds(w, 1), :], edge[wu][:, :], ACT.Copy).then_inc(adj_hi, 1)

            tiles(act, window_act)
            adj_high(NT - 1, 1)

            def gnn_exp(t, u, i, s):
                act.wait_ge(neg_ready, t + 1)
                act.activation(neg[:, :], neg[:, :], ACT.Exp).then_inc(neg_exp, 1)

            with act.Fori(0, NT) as t:
                gnn_exp(t, 0, None, 0)

            for kh in range(2):
                def k_turn(c):
                    for b, n in enumerate((4, 4, 2)):
                        q = 12 * kh + 3 * c + b
                        act.wait_ge(kt_mm, q + 1)
                        act.activation(kv[0][0][:, 4 * b:4 * b + n, c * P:(c + 1) * P],
                                       ps[:, 6 + q % 2, 0:n * P].rearrange("p (k n) -> p k n", k=n), ACT.Copy, scale=K_UP).then_inc(kt_hi, 1)

                for c in range(4):
                    u, q = c % 2, 4 * kh + c
                    for s in range(2):
                        conv_act(act, J_K[kh] + 1, c, s)
                    act.wait_ge(km_ready, q + 1)
                    act.wait_ge(ke_zero, 4)
                    if q >= 2:
                        act.wait_ge(kt_mm, 3 * (q - 1))
                    act.activation(k_exp[u][:, 0:N], banks(3 * ((c + kh) % 2), 3)[:, 0:N], ACT.Exp, bias=kmax[:, u, 1:2],
                                   scale=1.0 / (X_UP * W_UP), accum_out=ks[:, q:q + 1]).then_inc(ke_ready, 1)
                    if c:
                        k_turn(c - 1)

                def v_high(t, u, i, s):
                    if i is not None:
                        conv_act(act, J_V[kh] + 1, i, s)
                    act.wait_ge(g_done, G_BASE[J_V[kh]] + t + 1)
                    act.activation(kv[1][0][:, ds(t, 1), :], ps[:, BANK[J_V[kh]] + u, :], ACT.Copy, scale=H_UP / (X_UP * W_UP)).then_inc(g_hi, 1)
                    if isinstance(t, int) and t == 0:
                        k_turn(3)

                tiles(act, v_high)
                act.wait_ge(ctx_mm, 4 * (kh + 1))
                for b in range(2):
                    r = slice(64 * b, 64 * b + 64)
                    act.activation(ctxt[0][r, 4 * kh:4 * kh + 4, r], ps[r, 2 + 3 * kh, :].rearrange("p (k n) -> p k n", k=4)[:, :, r],
                                   ACT.Copy, scale=C_UP / (H_UP * K_UP)).then_inc(ctx_hi, 1)

            for qh in range(2):
                def q_turn(t, u):
                    act.wait_ge(q_mm, NT * qh + t + 1)
                    act.activation(qt[0][:, 4 * qh:4 * qh + 4, ds(t * P, P)], ps[:, 6 + u, :].rearrange("p (k n) -> p k n", k=4),
                                   ACT.Copy, scale=Q_UP).then_inc(q_hi, 1)

                def q_body(t, u, i, s):
                    if i is not None and qh == 0:
                        conv_act(act, J_Q + 1, i, s)
                    if i is not None and qh == 1:
                        for b in range(2):
                            pconv_act(act, 2 * i + s, b)
                    act.wait_ge(g_free, G_BASE[J_Q + qh] + t + 3)
                    act.activation(q_s[u][:, :], q_s[u][:, :], ACT.Exp, scale=1.0 / (X_UP * W_UP)).then_inc(q_exp, 1)
                    if not (isinstance(t, int) and t == 0):
                        q_turn(t - 1, 1 - u)
                    if i is not None and qh == 1:
                        c = 2 * i + s
                        for b in range(2):
                            act.wait_ge(m_mm, 2 * c + b + 1)
                            act.wait_ge(rks_ready, 1)
                            act.activation(m_sb[0][:, ds(c, 1), b * HALF:(b + 1) * HALF], ps[:, b, :], ACT.Copy,
                                           scale=rks[:, ds(c, 1)]).then_inc(m_hi, 1)

                tiles(act, q_body)
                q_turn(NT - 1, 1)

            def mix_act(t, u, i, s):
                n = turns(t, u, i, s)
                if i is not None:
                    fconv_act(act, i, s)
                act.wait_ge(ln2_mv, t + 1)
                act.activation(sd[:, u, :], mv[:, u, 1:2], ACT.Sqrt, bias=eps_ln[:, 0:1]).then_inc(ln2_sd, 1)
                act.wait_ge(ln2_nb, t + 1)
                act.wait_ge(xf_mm, 2 * t + 2)
                act.wait_ge(xf_st[u], 16 * n)
                act.activation(xfm[u][:, :], x2m[u][:, :], ACT.Identity, bias=nbias[:, u, :], scale=rstd[:, u, :]).then_inc(act_m, 1)
                act.wait_ge(act_m, 2 * t + 1)
                act.activation(sqj[:, :], xfm[u][:, :], ACT.Square, accum_out=ssq[:, 0:1]).then_inc(act_m, 1)
                act.wait_ge(act_m, 2 * t + 2)
                act.activation(ssq[:, 1:2], ssq[:, 0:1], ACT.Sqrt, bias=eps_rms[:, 0:1], scale=1.0 / D).then_inc(rms_sd, 1)
                for b in range(2):
                    act.wait_ge(xf_mm, 2 * t + b + 5)
                    if not (isinstance(t, int) and t == 0):
                        act.wait_ge(lg_mm, t)
                    act.activation(xft[:, 4 * b:4 * b + 4, :], ps[:, 4 + b, :].rearrange("p (k n) -> p k n", k=4), ACT.Copy).then_inc(xft_ready, 1)

            tiles(act, mix_act)
            act.wait_ge(wd_ready, 1)
            act.activation(wexp[:, :], wdiff[:, :], ACT.Exp).then_inc(we_ready, 1)
            for c in range(KD, NC):
                econv_act(act, 0, 0, c, c % 4)

            s_reg = act.alloc_register("act_slot")

            def xgt_high(s):
                for b in range(2):
                    act.wait_ge(xg_mm, 2 * s + b + 1)
                    act.activation(xgt[0][:, 4 * b:4 * b + 4, :], ps[:, b, :].rearrange("p (k n) -> p k n", k=4), ACT.Copy,
                                   scale=F_UP).then_inc(xgt_hi, 1)

            def hidt_high(s):
                act.wait_ge(hid_mm, s + 1)
                act.activation(hidt[0][:, :, :], ps[:, 6, :].rearrange("p (k n) -> p k n", k=KF), ACT.Copy).then_inc(hidt_hi, 1)

            def store_y(s):
                act.wait_ge(y_ready, s + 1)
                act.dma_start(y_dram[ds(s * P, P), :], y_sb[:, :]).then_inc(y_st, 16)

            def slot_act(s, e, slot, first, convert, very_first=False):
                if not very_first:
                    hidt_high(s - 1)
                if convert:
                    for c in range(KD):
                        if c == 0 and not very_first:
                            act.wait_ge(g1_done, s)
                        econv_act(act, e + 1, 1 - slot, c, c % 4)
                act.wait_ge(g1_done, s + 1)
                act.wait_ge(ab_done, 2 * s + 1)
                act.activation(ga[:, :], ga[:, :], ACT.Silu).then_inc(silu_done, 1)
                xgt_high(s + 1)
                if not very_first:
                    store_y(s - 1)
                if convert:
                    for c in range(KD, NC):
                        if c == KD and not very_first:
                            act.wait_ge(g2_done, s)
                        econv_act(act, e + 1, 1 - slot, c, c % 4)

            act.wait_ge(lg_ready, NT)
            for u in range(2):
                act.wait_ge(xf_st[u], 16 * (NT // 2 + 1))
                act.wait_ge(x2_st[u], 16 * (NT // 2 + 1))
            act.wait_ge(pos_ready, 1)
            xgt_high(0)

            def expert_act(e, slot, first=False, last=False):
                n = act.value_load(toti[0:1, 1, ds(e, 1)], min_val=1, max_val=NT)
                if first:
                    slot_act(0, e, slot, True, not last, very_first=True)
                    act.reg_mov(s_reg, 1)
                else:
                    slot_act(act.snap(s_reg, min_val=1, max_val=SLOTS - 1), e, slot, True, not last)
                    act.reg_add(s_reg, s_reg, 1)
                with act.If(n > 1):
                    with act.Fori(1, n):
                        slot_act(act.snap(s_reg, min_val=1, max_val=SLOTS - 1), e, slot, False, False)
                        act.reg_add(s_reg, s_reg, 1)

            expert_act(0, 0, first=True)
            expert_act(1, 1)
            with act.Fori(1, NE // 2 - 1) as j:
                expert_act(2 * j, 0)
                expert_act(2 * j + 1, 1)
            expert_act(NE - 2, 0)
            expert_act(NE - 1, 1, last=True)
            s_end = act.snap(s_reg, min_val=1, max_val=SLOTS)
            hidt_high(s_end - 1)
            store_y(s_end - 1)

        @block.tensor
        def _(pe):
            pe.wait_ge(const_set, 19)
            pe.sem_inc(xt_done, 4)
            pe.sem_inc(g_free, 2)
            for s_ in (cnt_ready, gnn_free, x2_ready, qt_done):
                pe.sem_inc(s_, 2)
            pe.sem_inc(oh_free, UNIT)

            def ranges_in():
                pe.wait_ge(idx_ready, 1)
                for q in range(2):
                    for g in range(EG):
                        mm = pe.matmul(ps[0:16, 6 + q, g * P:(g + 1) * P], urep[:, q, g, :], ident[:, :], start=True, stop=True)
                mm.then_inc(win_mm, 1)

            def ranges_out():
                pe.wait_ge(win_ready, 1)
                for q in range(2):
                    mm = pe.matmul(ps[0:1, 6, 16 * q:16 * q + 16], win[0:16, q:q + 1], ident[0:16, 0:16], start=True, stop=True)
                mm.then_inc(win_mm, 1)

            def turn_x(t, u):
                pe.wait_ge(xn_ready, t + 1)
                pe.wait_ge(xt_done, 2 * t + 2)
                for b in range(2):
                    for k in range(4):
                        mm = pe.transpose(ps[:, 2 * u + b, k * P:(k + 1) * P], x_n[u][:, (4 * b + k) * P:(4 * b + k + 1) * P], ident[:, :])
                    mm.then_inc(xn_turned, 1)

            def gemm(j, t, u):
                g = G_BASE[j] + t
                pe.wait_ge(g_free, g + 1)
                for k in range(KD):
                    mm = split_mm(pe, [ps[:, BANK[j] + u, :]], [xt[p][:, k, ds(t * P, P)] for p in range(2)],
                                  [[w_sb[j % 2][p][:, k, :] for p in range(2)]], k == 0, k == KD - 1)
                mm.then_inc(g_done, 1)
                return mm

            turn_x(0, 0)
            for half in range(2):
                pe.wait_ge(w_done, KD * (half + 1) + 2)

                def h_body(t, u, i, s):
                    if half == 0:
                        if not (isinstance(t, int) and t == NT - 1):
                            turn_x(t + 1, 1 - u)
                        pe.wait_ge(xt_done, 2 * t + 6)
                    gemm(half, t, u)
                    if half == 1 and isinstance(t, int):
                        ranges_in() if t == 0 else ranges_out()

                tiles(pe, h_body)
            pe.wait_ge(alrep_ready, 1)
            for t in range(NT):
                mm = pe.matmul(banks(0, 3)[:, t * P:(t + 1) * P], al_rep[:, t, :], ident[:, :], start=True, stop=True, skip_group_check=True)
            mm.then_inc(alrow_mm, 1)
            r = pe.alloc_register("pe_units")
            pe.reg_mov(r, 0)
            pe.wait_ge(alrow_ready, 1)
            pe.wait_ge(win_ready, 2)
            pe.wait_ge(g_free, 22)
            chunks = ((0, 0, HALF), (1, HALF, HALF), (2, 2 * HALF, NP - 2 * HALF))

            def window_pe(w, wu, i, s_):
                pe.wait_ge(cnt_ready, w + 1)
                steps = pe.value_load(lohi[0:1, ds(16 + w, 1)], min_val=MIN_STEPS, max_val=ER)
                for b, c0, n in chunks:
                    pe.matmul(ps[:, 3 * wu + b, 0:n], zero_h[:, 0:P], zero_h[:, 0:n], start=True, stop=False, skip_group_check=True)
                with pe.Fori(0, steps):
                    n_u = pe.snap(r, min_val=0, max_val=NT * ER)
                    for u in range(UNIT):
                        pe.wait_ge(oh_ready, UNIT * n_u + u + 1)
                        for b, c0, n in chunks:
                            n = min(n, N - c0)
                            mm = pe.matmul(ps[:, 3 * wu + b, 0:n], oh_dst[u][:, :], oh_src[u][:, c0:c0 + n],
                                           start=False, stop=False, skip_group_check=True)
                        mm.then_inc(oh_free, 1)
                    pe.reg_add(r, r, 1)
                pe.matmul(ps[:, 3 * wu + 2, 0:2], zero_h[:, 0:P], zero_h[:, 0:2], start=False, stop=True,
                          skip_group_check=True).then_inc(win_done, 1)

            tiles(pe, window_pe)
            pe.wait_ge(adj_done, NT + 2)

            def gnn(t, u):
                pe.wait_ge(gnn_free, t + 1)
                for k in range(NT):
                    lhs = [adj[p][:, k, ds(t * P, P)] for p in range(2)]
                    split_mm(pe, [ps[:, 2 * u + b, :] for b in range(2)], lhs,
                             [[h[p][:, k, b * HALF:(b + 1) * HALF] for p in range(2)] for b in range(2)], k == 0, k == NT - 1)
                    for p in range(2):
                        mm = pe.matmul(ps[:, 4 + u, 0:2], lhs[p], ones_h[:, :], start=(k == 0 and p == 0), stop=(k == NT - 1 and p == 1),
                                       skip_group_check=True)
                mm.then_inc(gnn_done, 1)

            tiles(pe, lambda t, u, i, s: gnn(t, u))

            for kh in range(2):
                j = J_K[kh]

                def k_turn(c):
                    pe.wait_ge(ke_ready, 4 * kh + c + 1)
                    t0 = 0
                    for b, n in enumerate((4, 4, 2)):
                        q = 12 * kh + 3 * c + b
                        if q >= 2:
                            pe.wait_ge(kt_done, q - 1)
                        for k in range(n):
                            mm = pe.transpose(ps[:, 6 + q % 2, k * P:(k + 1) * P], k_exp[c % 2][:, (t0 + k) * P:(t0 + k + 1) * P], ident[:, :])
                        mm.then_inc(kt_mm, 1)
                        t0 += n

                pe.wait_ge(w_done, KD * (j + 1) + 2)
                for c in range(4):
                    bank = 3 * ((c + kh) % 2)
                    if kh == 0 and c == 0:
                        pe.wait_ge(gnn_free, NT + 2)
                    if kh == 1 and c == 0:
                        pe.wait_ge(ke_ready, 4)
                    if kh == 1 and c == 1:
                        pe.wait_ge(ctx_done, 2)
                        pe.wait_ge(g_free, G_BASE[J_V[0]] + NT + 2)
                    if c >= 2:
                        pe.wait_ge(ke_ready, 4 * kh + c - 1)
                    for k in range(KD):
                        lhs = [w_sb[j % 2][p][:, k, c * P:(c + 1) * P] for p in range(2)]
                        mm = split_mm(pe, [ps[:, bank + b, 0:n] for b, c0, n in chunks], lhs,
                                      [[xt[p][:, k, c0:c0 + n] for p in range(2)] for b, c0, n in chunks], k == 0, k == KD - 1)
                    mm.then_inc(k_done, 1)
                    if c:
                        k_turn(c - 1)

                def v_body(t, u, i, s):
                    gemm(J_V[kh], t, u)
                    if isinstance(t, int) and t == 0:
                        k_turn(3)

                pe.wait_ge(w_done, KD * (J_V[kh] + 1) + 2)
                pe.wait_ge(ke_ready, 4 * kh + 3)
                tiles(pe, v_body)
                pe.wait_ge(kt_done, 12 * kh + 12)
                pe.wait_ge(g_free, G_BASE[J_V[kh]] + NT + 2)
                with pe.Fori(0, 4) as c:
                    for t in range(NT):
                        mm = split_mm(pe, [ps[:, 2 + 3 * kh, ds(c * P, P)]], [kv[1][p][:, t, ds(c * P, P)] for p in range(2)],
                                      [[kv[0][p][:, t, ds(c * P, P)] for p in range(2)]], t == 0, t == NT - 1)
                    mm.then_inc(ctx_mm, 1)

            def project(c):
                for b in range(2):
                    pe.wait_ge(w_done, KD * J_P + 2 * c + b + 3)
                    pe.wait_ge(m_done, 2 * c + b + 1)
                    split_mm(pe, [ps[:, b, :]], [ctxt[p][:, ds(c, 1), :] for p in range(2)],
                             [[w_proj[b][p][:, ds(c, 1), :] for p in range(2)]], True, True).then_inc(m_mm, 1)

            for qh in range(2):
                if qh == 1:
                    pe.wait_ge(ctx_done, 4)
                pe.wait_ge(w_done, KD * (J_Q + qh + 1) + 2)

                def q_turn(t, u):
                    g = NT * qh + t
                    pe.wait_ge(q_norm, g + 1)
                    pe.wait_ge(qt_done, g + 1)
                    for k in range(4):
                        mm = pe.transpose(ps[:, 6 + u, k * P:(k + 1) * P], q_s[u][:, k * P:(k + 1) * P], ident[:, :])
                    mm.then_inc(q_mm, 1)

                def q_body(t, u, i, s):
                    gemm(J_Q + qh, t, u)
                    if not (isinstance(t, int) and t == 0):
                        q_turn(t - 1, 1 - u)
                    if i is not None and qh == 1:
                        project(2 * i + s)

                tiles(pe, q_body)
                q_turn(NT - 1, 1)
                pe.wait_ge(qt_done, NT * (qh + 1) + 2)
            pe.wait_ge(m_done, 2 * KD + 2)
            pe.wait_ge(g_free, G_BASE[J_Q + 1] + NT + 2)

            def mix(t, u):
                pe.wait_ge(x2_ready, t + 1)
                for c in range(KD):
                    mm = split_mm(pe, [ps[:, 2 * u + b, :] for b in range(2)], [qt[p][:, c, ds(t * P, P)] for p in range(2)],
                                  [[m_sb[p][:, c, b * HALF:(b + 1) * HALF] for p in range(2)] for b in range(2)], c == 0, c == KD - 1)
                mm.then_inc(mix_done, 1)

            def route(t, u):
                pe.wait_ge(xf_ready, t + 1)
                for b in range(2):
                    if not (isinstance(t, int) and t == 0):
                        pe.wait_ge(xft_ready, 2 * t)
                    for k in range(4):
                        mm = pe.transpose(ps[:, 4 + b, k * P:(k + 1) * P], xfm[u][:, (4 * b + k) * P:(4 * b + k + 1) * P], ident[:, :])
                    mm.then_inc(xf_mm, 1)
                pe.wait_ge(xft_ready, 2 * t + 2)
                if not (isinstance(t, int) and t == 0):
                    pe.wait_ge(lg_ready, t)
                for k in range(KD):
                    mm = pe.matmul(ps[:, 6, 0:NE], xft[:, k, :], wg_sb[:, k, :], start=(k == 0), stop=(k == KD - 1))
                mm.then_inc(lg_mm, 1)

            def mix_body(t, u, i, s):
                mix(t, u)
                if not (isinstance(t, int) and t == 0):
                    route(t - 1, 1 - u)

            tiles(pe, mix_body)
            route(NT - 1, 1)
            pe.wait_ge(mask_ready, 1)
            pe.matmul(ps[:, 7, 0:NT * NE], tri[:, :], mask[:, :, :].rearrange("p t e -> p (t e)"), start=True, stop=False, skip_group_check=True)
            pe.matmul(ps[:, 7, 0:NT * NE], ones_b[:, :], before[:, 0:NT, :].rearrange("p t e -> p (t e)"), start=False, stop=True, skip_group_check=True)
            pe.matmul(ps[:, 7, 128:128 + NE], ones_b[:, :], before[:, NT, :], start=True, stop=True, skip_group_check=True).then_inc(rank_mm, 1)

            for q in range(TOPK * NT):
                pe.wait_ge(place_ready, q + 1)
                mm = pe.matmul(ps[:, 7, 256:256 + SLOTS + 1], oh_row[:, q, :], oh_tile[:, q, :], start=(q == 0), stop=(q == TOPK * NT - 1),
                               skip_group_check=True)
            mm.then_inc(place_mm, 1)

            s_reg = pe.alloc_register("pe_slot")

            def turn_g(s):
                pe.wait_ge(xg_ld, 16 * (s + 1))
                if not (isinstance(s, int) and s == 0):
                    pe.wait_ge(xgt_done, 2 * s)
                for b in range(2):
                    for k in range(4):
                        mm = pe.transpose(ps[:, b, k * P:(k + 1) * P], xg[:, (4 * b + k) * P:(4 * b + k + 1) * P], ident[:, :])
                    mm.then_inc(xg_mm, 1)

            def turn_hid(s):
                pe.wait_ge(hid_ready, s + 1)
                if not (isinstance(s, int) and s == 0):
                    pe.wait_ge(hidt_done, s)
                for k in range(KF):
                    mm = pe.transpose(ps[:, 6, k * P:(k + 1) * P], hid[:, k * P:(k + 1) * P], ident[:, :])
                mm.then_inc(hid_mm, 1)

            def up(s, slot):
                pe.wait_ge(xgt_done, 2 * s + 2)
                if not (isinstance(s, int) and s == 0):
                    pe.wait_ge(ab_done, 2 * s)
                for k in range(KD):
                    mm = split_mm(pe, [ps[:, 2 + b, :] for b in range(2)], [xgt[p][:, k, :] for p in range(2)],
                                  [[ew[slot][p][:, k, b * HALF:(b + 1) * HALF] for p in range(2)] for b in range(2)], k == 0, k == KD - 1)
                mm.then_inc(g1_done, 1)

            def down(s, slot, e):
                pe.wait_ge(ew_done, NC * e + NC + 4)
                pe.wait_ge(hidt_done, s + 1)
                if not (isinstance(s, int) and s == 0):
                    pe.wait_ge(y_ready, s)
                for k in range(KF):
                    mm = split_mm(pe, [ps[:, 4 + b, :] for b in range(2)], [hidt[p][:, k, :] for p in range(2)],
                                  [[ew[slot][p][:, KD + k, b * HALF:(b + 1) * HALF] for p in range(2)] for b in range(2)], k == 0, k == KF - 1)
                mm.then_inc(g2_done, 1)

            turn_g(0)

            def expert_pe(e, slot, first=False):
                n = pe.value_load(toti[0:1, 1, ds(e, 1)], min_val=1, max_val=NT)
                pe.wait_ge(ew_done, NC * e + KD + 4)
                if first:
                    turn_g(1)
                    up(0, slot)
                    pe.reg_mov(s_reg, 1)
                else:
                    s = pe.snap(s_reg, min_val=1, max_val=SLOTS - 1)
                    turn_g(s + 1)
                    turn_hid(s - 1)
                    up(s, slot)
                    down(s - 1, 1 - slot, e - 1)
                    pe.reg_add(s_reg, s_reg, 1)
                with pe.If(n > 1):
                    with pe.Fori(1, n):
                        s = pe.snap(s_reg, min_val=1, max_val=SLOTS - 1)
                        turn_g(s + 1)
                        turn_hid(s - 1)
                        up(s, slot)
                        down(s - 1, slot, e)
                        pe.reg_add(s_reg, s_reg, 1)

            expert_pe(0, 0, first=True)
            expert_pe(1, 1)
            with pe.Fori(1, NE // 2) as j:
                expert_pe(2 * j, 0)
                expert_pe(2 * j + 1, 1)
            s_end = pe.snap(s_reg, min_val=1, max_val=SLOTS)
            turn_hid(s_end - 1)
            down(s_end - 1, 1, NE - 1)

        @block.vector
        def _(dve):
            dve.sem_inc(adj_done, 2)
            dve.sem_inc(m_done, 2)

            def chain(s, per):
                state = {"n": 0}

                def start(r):
                    state["r"], state["n"] = r, 0

                def link(ins):
                    state["n"] += 1
                    assert state["n"] <= per
                    ins.then_inc(s, 1)
                    dve.wait_ge(s, state["r"] * per + state["n"])
                return start, link

            def ln_stats(t, u, n):
                dve.wait_ge(xin_ld[u], 16 * n)
                r = 2 * t
                for b in range(2):
                    ins = dve.bn_stats(stats[:, u, 6 * b:6 * b + 6], x_in[u][:, b * HALF:(b + 1) * HALF])
                ins.then_inc(dve_ln, 1)
                wait_alone(dve, dve_ln, r + 1)
                dve.bn_aggr(mv[:, u, :], stats[:, u, :]).then_inc(ln_mv, 1)
                dve.wait_ge(ln_mv, t + 1)
                dve.wait_ge(ln_sd, t + 1)
                dve.reciprocal(rstd[:, u, :], sd[:, u, :]).then_inc(dve_ln, 1)
                dve.wait_ge(dve_ln, r + 2)
                dve.scalar_tensor_tensor(nbias[:, u, :], mv[:, u, 0:1], -1.0, rstd[:, u, :], ALU.mult, ALU.mult).then_inc(ln_nb, 1)

            def xt_low(t, u):
                for b in range(2):
                    dve.wait_ge(xt_hi, 2 * t + b + 1)
                    o = slice(4 * b, 4 * b + 4)
                    dve.scalar_tensor_tensor(xt[1][:, o, ds(t * P, P)], ps[:, 2 * u + b, :].rearrange("p (k n) -> p k n", k=4), X_UP,
                                             xt[0][:, o, ds(t * P, P)], ALU.mult, ALU.subtract).then_inc(xt_done, 1)

            start, link = chain(dve_c, 100)

            def indices():
                start(0)
                dve.wait_ge(const_ld, 16 * 9)
                dve.wait_ge(const_set, 19)
                dve.tensor_copy(src_f[:, :], idx_in[:, 0, :])
                dve.tensor_copy(dst_f[:, :], idx_in[:, 1, :])
                link(dve.tensor_copy(rows_f[:, :, :], rows_i[:, :, :]))
                dve.tensor_reduce(ured[:, 0, :], rows_f[:, :, :], AX, ALU.min)
                link(dve.tensor_reduce(ured[:, 1, :], rows_f[:, :, :], AX, ALU.max))
                for q in range(2):
                    for g in range(EG):
                        ins = dve.tensor_scalar(urep[:, q, g, :], ones_f[:, 0:16], ured[:, q, g:g + 1], None, ALU.mult)
                ins.then_inc(idx_ready, 1)

            def ranges():
                dve.wait_ge(win_mm, 1)
                mn, mx = ps[0:16, 6, 0:ER], ps[0:16, 7, 0:ER]
                link(dve.tensor_scalar(win[:, 2:3], iota_w[:, 0:1], float(P), None, ALU.add))
                link(dve.tensor_scalar(rtile[:, 1, :], mn, win[:, 2:3], None, ALU.is_lt))
                link(dve.scalar_tensor_tensor(rtile[:, 2, :], mx, iota_w[:, 0:1], rtile[:, 1, :], ALU.is_ge, ALU.mult))
                link(dve.scalar_tensor_tensor(rtile[:, 1, :], iota_u[:, :], -BIG, rtile[:, 2, :], ALU.add, ALU.mult))
                link(dve.scalar_tensor_tensor(rtile[:, 3, :], iota_u[:, :], 1.0, rtile[:, 2, :], ALU.add, ALU.mult))
                link(dve.tensor_reduce(win[:, 3:4], rtile[:, 1, :], AX, ALU.min))
                link(dve.tensor_reduce(win[:, 4:5], rtile[:, 3, :], AX, ALU.max))
                link(dve.tensor_scalar(win[:, 5:6], win[:, 3:4], BIG, None, ALU.add))
                link(dve.tensor_scalar(win[:, 0:1], win[:, 5:6], float(ET - MIN_STEPS * UNIT), None, ALU.min))
                link(dve.tensor_tensor(win[:, 6:7], win[:, 4:5], win[:, 0:1], ALU.subtract))
                link(dve.tensor_scalar(win[:, 7:8], win[:, 6:7], float(UNIT - 1), None, ALU.add))
                link(dve.tensor_scalar(win[:, 6:7], win[:, 7:8], float(UNIT * MIN_STEPS), None, ALU.max))
                link(dve.tensor_copy(wini[:, 0:1], win[:, 6:7]))
                link(dve.tensor_scalar(wini[:, 1:2], wini[:, 0:1], UNIT.bit_length() - 1, None, ALU.arith_shift_right))
                dve.tensor_copy(win[:, 1:2], wini[:, 1:2]).then_inc(win_ready, 1)

            def h_low(half):
                def body(t, u, i, s):
                    if half == 0 and not (isinstance(t, int) and t == NT - 1):
                        xt_low(t + 1, 1 - u)
                    if half == 0 and not (isinstance(t, int) and t > NT - 3):
                        ln_stats(t + 2, u, turns(t, u, i, s) + 1)
                    if i is not None:
                        conv_dve(dve, half + 1, i, s)
                    c = slice(half * HALF, (half + 1) * HALF)
                    dve.wait_ge(g_hi, G_BASE[half] + t + 1)
                    dve.scalar_tensor_tensor(h[1][:, ds(t, 1), c], ps[:, 4 + u, :], H_UP / (X_UP * W_UP), h[0][:, ds(t, 1), c],
                                             ALU.mult, ALU.subtract)
                    dve.wait_ge(g_free, G_BASE[half] + t + 2)
                    for q in range(2):
                        ins = dve.scalar_tensor_tensor(junk[q][:, :], ps[:, 4 + u, :], 1.0 / (X_UP * W_UP), a_b[:, q, c], ALU.mult, ALU.mult,
                                                       accum_out=al_part[:, q, half, ds(t, 1)])
                    ins.then_inc(g_free, 1)
                    if half == 1 and isinstance(t, int) and t == 0:
                        ranges()
                return body

            dve.wait_ge(const_set, 19)
            ln_stats(0, 0, 1)
            for g in range(KD // 2):
                dve.wait_ge(w_hi, 2 * g + 2)
                dve.scalar_tensor_tensor(w_sb[0][1][:, 2 * g:2 * g + 2, :], stage_h[:, 2 * g:2 * g + 2, :], W_UP,
                                         w_sb[0][0][:, 2 * g:2 * g + 2, :], ALU.mult, ALU.subtract).then_inc(w_done, 2)
                if g == 1:
                    xt_low(0, 0)
                    ln_stats(1, 1, 1)
            tiles(dve, h_low(0), 3)
            indices()
            tiles(dve, h_low(1))
            dve.wait_ge(g_free, 22)
            link(dve.tensor_tensor(al_ar[:, :, :], al_part[:, :, 0, :], al_part[:, :, 1, :], ALU.add))
            dve.tensor_copy(al_rep[:, :, :], al_ar[:, 0, :].to_broadcast([P, NT, P])).then_inc(alrep_ready, 1)
            dve.wait_ge(win_mm, 2)
            dve.tensor_copy(lohi[0:1, :], ps[0:1, 6, 0:32]).then_inc(win_ready, 1)

            r, tile_r = dve.alloc_register("dve_steps"), dve.alloc_register("dve_tile")
            dve.reg_mov(r, 0)
            dve.wait_ge(win_ready, 2)

            def one_hots(w):
                first = dve.snap(tile_r, min_val=0, max_val=ET - UNIT)
                n_u = dve.snap(r, min_val=0, max_val=NT * ER)
                for u in range(UNIT):
                    dve.wait_ge(oh_free, UNIT * n_u + u + 1)
                    dve.tensor_scalar(oh_src[u][:, 0:N], iota_n[:, 0:N], src_f[:, ds(first + u, 1)], None, ALU.is_equal)
                    dve.tensor_scalar(oh_dst[u][:, :], iota_n[:, ds(w * P, P)], dst_f[:, ds(first + u, 1)], None,
                                      ALU.is_equal).then_inc(oh_ready, 1)
                dve.reg_add(r, r, 1)
                dve.reg_add(tile_r, tile_r, UNIT)

            def weigh(w, wu):
                dve.wait_ge(e_ready, w + 1)
                dve.wait_ge(win_done, w + 1)
                dve.tensor_tensor(edge[wu][:, :], edge[wu][:, :], banks(3 * wu, 3)[:, 0:NP], ALU.mult).then_inc(cnt_ready, 1)

            def adj_low(w, wu):
                dve.wait_ge(adj_hi, w + 1)
                dve.wait_ge(cnt_ready, w + 3)
                dve.tensor_tensor(adj[1][:, ds(w, 1), :], edge[wu][:, :], adj[0][:, ds(w, 1), :], ALU.subtract).then_inc(adj_done, 1)

            def window_dve(w, wu, i, s_):
                lo = dve.value_load(lohi[0:1, ds(w, 1)], min_val=0, max_val=ER - 1)
                steps = dve.value_load(lohi[0:1, ds(16 + w, 1)], min_val=MIN_STEPS, max_val=ER)
                dve.reg_mov(tile_r, lo)
                one_hots(w)
                if not (isinstance(w, int) and w == 0):
                    weigh(w - 1, 1 - wu)
                with dve.Fori(1, steps):
                    one_hots(w)
                if not (isinstance(w, int) and w == 0):
                    adj_low(w - 1, 1 - wu)

            tiles(dve, window_dve)
            weigh(NT - 1, 1)
            adj_low(NT - 1, 1)

            def gnn(t, u, i, s):
                start, link = chain(dve_g, 5)
                start(t)
                dve.wait_ge(gnn_done, t + 1)
                link(dve.tensor_scalar(rsum[:, u, 0:1], ps[:, 4 + u, 0:1], EPS_GNN, None, ALU.add))
                link(dve.reciprocal(rsum[:, u, 1:2], rsum[:, u, 0:1]))
                link(dve.tensor_scalar(rsum[:, u, 2:3], rsum[:, u, 1:2], 1.0 / H_UP, None, ALU.mult))
                dve.tensor_scalar(neg[:, :], banks(2 * u, 2), rsum[:, u, 2:3], 0.0, ALU.mult, ALU.min).then_inc(neg_ready, 1)
                dve.tensor_scalar(poz[:, :], banks(2 * u, 2), rsum[:, u, 2:3], 0.0, ALU.mult, ALU.max).then_inc(gnn_free, 1)
                dve.wait_ge(x1_ld[u], 16 * turns(t, u, i, s))
                link(dve.tensor_tensor(x1[u][:, :], x1[u][:, :], bproj_b[:, :], ALU.add))
                dve.wait_ge(gnn_free, t + 3)
                link(dve.tensor_tensor(x1[u][:, :], x1[u][:, :], poz[:, :], ALU.add))
                dve.wait_ge(neg_exp, t + 1)
                dve.scalar_tensor_tensor(x1[u][:, :], neg[:, :], -1.0, x1[u][:, :], ALU.add, ALU.add).then_inc(x1_ready, 1)

            tiles(dve, gnn)

            for kh in range(2):
                def k_turn(c):
                    for b, n in enumerate((4, 4, 2)):
                        q = 12 * kh + 3 * c + b
                        o = (slice(None), slice(4 * b, 4 * b + n), slice(c * P, (c + 1) * P))
                        dve.wait_ge(kt_hi, 3 * (4 * kh + c) + b + 1)
                        dve.scalar_tensor_tensor(kv[0][1][o], ps[:, 6 + q % 2, 0:n * P].rearrange("p (k n) -> p k n", k=n), K_UP,
                                                 kv[0][0][o], ALU.mult, ALU.subtract).then_inc(kt_done, 1)

                for c in range(4):
                    u, q = c % 2, 4 * kh + c
                    for s in range(2):
                        conv_dve(dve, J_K[kh] + 1, c, s)
                    dve.wait_ge(k_done, q + 1)
                    dve.tensor_reduce(kmax[:, u, 0:1], banks(3 * ((c + kh) % 2), 3)[:, 0:N], AX, ALU.max).then_inc(dve_k, 1)
                    dve.wait_ge(dve_k, q + 1)
                    dve.tensor_scalar(kmax[:, u, 1:2], kmax[:, u, 0:1], -1.0 / (X_UP * W_UP), None, ALU.mult).then_inc(km_ready, 1)
                    if c:
                        k_turn(c - 1)

                def v_low(t, u, i, s):
                    if i is not None:
                        conv_dve(dve, J_V[kh] + 1, i, s)
                    dve.wait_ge(g_hi, 20 + NT * kh + t + 1)
                    dve.scalar_tensor_tensor(kv[1][1][:, ds(t, 1), :], ps[:, BANK[J_V[kh]] + u, :], H_UP / (X_UP * W_UP), kv[1][0][:, ds(t, 1), :],
                                             ALU.mult, ALU.subtract).then_inc(g_free, 1)
                    if isinstance(t, int) and t == 0:
                        k_turn(3)

                tiles(dve, v_low)
                for b in range(2):
                    r_ = slice(64 * b, 64 * b + 64)
                    dve.wait_ge(ctx_hi, 2 * kh + 2)
                    dve.scalar_tensor_tensor(ctxt[1][r_, 4 * kh:4 * kh + 4, r_], ps[r_, 2 + 3 * kh, :].rearrange("p (k n) -> p k n", k=4)[:, :, r_],
                                             C_UP / (H_UP * K_UP), ctxt[0][r_, 4 * kh:4 * kh + 4, r_], ALU.mult, ALU.subtract).then_inc(ctx_done, 1)
            dve.wait_ge(ke_ready, 8)
            dve.reciprocal(rks[:, :], ks[:, :]).then_inc(rks_ready, 1)

            for qh in range(2):
                def q_turn(t, u):
                    o = (slice(None), slice(4 * qh, 4 * qh + 4), ds(t * P, P))
                    dve.wait_ge(q_hi, NT * qh + t + 1)
                    dve.scalar_tensor_tensor(qt[1][o], ps[:, 6 + u, :].rearrange("p (k n) -> p k n", k=4), Q_UP, qt[0][o],
                                             ALU.mult, ALU.subtract).then_inc(qt_done, 1)

                def q_body(t, u, i, s):
                    start, link = chain(dve_q, 3)
                    start(NT * qh + t)
                    if i is not None and qh == 0:
                        conv_dve(dve, J_Q + 1, i, s)
                    if i is not None and qh == 1:
                        for b in range(2):
                            pconv_dve(dve, 2 * i + s, b)
                    q3 = ps[:, BANK[J_Q] + u, :].rearrange("p (h d) -> p h d", d=64)
                    s3 = q_s[u][:, :].rearrange("p (h d) -> p h d", d=64)
                    dve.wait_ge(g_done, G_BASE[J_Q + qh] + t + 1)
                    link(dve.tensor_reduce(qred[:, u, 0, :], q3, AX, ALU.max))
                    dve.tensor_tensor(s3, q3, qred[:, u, 0, :].to_broadcast([P, 8, 64]), ALU.subtract).then_inc(g_free, 1)
                    dve.wait_ge(q_exp, NT * qh + t + 1)
                    link(dve.tensor_reduce(qred[:, u, 1, :], s3, AX, ALU.add))
                    link(dve.reciprocal(qred[:, u, 2, :], qred[:, u, 1, :]))
                    dve.tensor_tensor(s3, s3, qred[:, u, 2, :].to_broadcast([P, 8, 64]), ALU.mult).then_inc(q_norm, 1)
                    if not (isinstance(t, int) and t == 0):
                        q_turn(t - 1, 1 - u)
                    if i is not None and qh == 1:
                        c = 2 * i + s
                        for b in range(2):
                            o = (slice(None), ds(c, 1), slice(b * HALF, (b + 1) * HALF))
                            dve.wait_ge(m_hi, 2 * c + b + 1)
                            dve.scalar_tensor_tensor(m_sb[1][o], ps[:, b, :], rks[:, ds(c, 1)], m_sb[0][o], ALU.mult, ALU.subtract).then_inc(m_done, 1)

                tiles(dve, q_body)
                q_turn(NT - 1, 1)

            def top2(t):
                start, link = chain(dve_m, 6)
                start(t)
                dve.wait_ge(lg_mm, t + 1)
                dve.tensor_tensor(lg[:, :], ps[:, 6, 0:NE], bg_b[:, :], ALU.add).then_inc(lg_ready, 1)
                wait_alone(dve, lg_ready, t + 1)
                link(dve.max(top8[:, :], lg[:, :]))
                dve.tensor_tensor(wdiff[:, ds(t, 1)], top8[:, 1:2], top8[:, 0:1], ALU.subtract)
                link(dve.max_index(idx8[:, :], top8[:, :], lg[:, :]))
                link(dve.tensor_copy(idxf[:, :], idx8[:, :]))
                for k in range(TOPK):
                    last = isinstance(t, int) and t == NT - 1
                    ins = dve.tensor_scalar(onehot[:, k, t, :] if isinstance(t, int) else onehot[:, k, ds(t, 1), :], iota_e[:, :], idxf[:, k:k + 1],
                                            valid[:, 0:1] if last else None, ALU.is_equal, ALU.mult if last else ALU.bypass)
                link(ins)
                link(dve.tensor_tensor(mask[:, ds(t, 1), :], onehot[:, 0, ds(t, 1), :], onehot[:, 1, ds(t, 1), :], ALU.add))
                link(dve.tensor_tensor(before[:, ds(t + 1, 1), :], before[:, ds(t, 1), :], mask[:, ds(t, 1), :], ALU.add))

            def mix(t, u, i, s):
                n = turns(t, u, i, s)
                if i is not None:
                    fconv_dve(dve, i, s)
                dve.wait_ge(mix_done, t + 1)
                dve.wait_ge(x1m_ld[u], 16 * n)
                dve.wait_ge(x2_st[u], 16 * n)
                dve.scalar_tensor_tensor(x2m[u][:, :], banks(2 * u, 2), 1.0 / (Q_UP * M_UP), x1m[u][:, :], ALU.mult, ALU.add).then_inc(x2_ready, 1)
                dve.wait_ge(x2_ready, t + 3)
                for b in range(2):
                    ins = dve.bn_stats(stats[:, u, 6 * b:6 * b + 6], x2m[u][:, b * HALF:(b + 1) * HALF])
                ins.then_inc(dve_x, 1)
                wait_alone(dve, dve_x, 3 * t + 1)
                dve.bn_aggr(mv[:, u, :], stats[:, u, :]).then_inc(ln2_mv, 1)
                dve.wait_ge(ln2_mv, t + 1)
                dve.wait_ge(ln2_sd, t + 1)
                dve.reciprocal(rstd[:, u, :], sd[:, u, :]).then_inc(dve_x, 1)
                dve.wait_ge(dve_x, 3 * t + 2)
                dve.scalar_tensor_tensor(nbias[:, u, :], mv[:, u, 0:1], -1.0, rstd[:, u, :], ALU.mult, ALU.mult).then_inc(ln2_nb, 1)
                dve.wait_ge(rms_sd, t + 1)
                dve.reciprocal(ssq[:, 2:3], ssq[:, 1:2]).then_inc(dve_x, 1)
                dve.wait_ge(dve_x, 3 * t + 3)
                dve.scalar_tensor_tensor(xfm[u][:, :], xfm[u][:, :], ssq[:, 2:3], lnw_b[:, :], ALU.mult, ALU.mult).then_inc(xf_ready, 1)
                if not (isinstance(t, int) and t == 0):
                    top2(t - 1)

            tiles(dve, mix)
            top2(NT - 1)
            dve.sem_inc(mask_ready, 1)

            start, link = chain(dve_r, 24)
            start(0)
            dve.sem_inc(wd_ready, 1)
            dve.wait_ge(rank_mm, 1)
            dve.tensor_copy(rank[:, :, :], ps[:, 7, 0:NT * NE].rearrange("p (t e) -> p t e", e=NE))
            link(dve.tensor_scalar(tot[:, 0, :], ps[:, 7, 128:128 + NE], float(P - 1), None, ALU.add))
            link(dve.tensor_copy(toti[:, 0, :], tot[:, 0, :]))
            link(dve.tensor_scalar(toti[:, 2, :], toti[:, 0, :], 7, None, ALU.arith_shift_right))
            link(dve.tensor_copy(tot[:, 1, :], toti[:, 2, :]))
            link(dve.tensor_scalar(tot[:, 2, :], tot[:, 1, :], 1.0, None, ALU.max))
            link(dve.tensor_tensor_scan(tot[:, 3, :], ones_f[:, 0:NE], tot[:, 2, :], 0.0, ALU.mult, ALU.add))
            link(dve.tensor_tensor(tot[:, 4, :], tot[:, 3, :], tot[:, 2, :], ALU.subtract))
            link(dve.tensor_scalar(tot[:, 5, :], tot[:, 4, :], float(P), None, ALU.mult))
            dve.tensor_copy(toti[:, 1, :], tot[:, 2, :])
            dve.tensor_copy(toti[:, 2, :], tot[:, 3, :])
            link(dve.tensor_tensor(rank[:, :, :], rank[:, :, :], tot[:, 5:6, :].to_broadcast([P, NT, NE]), ALU.add))
            for k in range(TOPK):
                link(dve.tensor_tensor(ranked[:, :, :], rank[:, :, :], onehot[:, k, :, :], ALU.mult))
                link(dve.tensor_reduce(posf[:, k, :], ranked[:, :, :], AX, ALU.add))
            link(dve.tensor_copy(pos[:, :, :], posf[:, :, :]))
            link(dve.tensor_scalar(tile_i[:, :, :], pos[:, :, :], 7, None, ALU.arith_shift_right))
            link(dve.tensor_copy(tile_f[:, :, :], tile_i[:, :, :]))
            dve.tensor_scalar(tok[:, NT - 1:NT], tok[:, NT - 1:NT], valid[:, 0:1], None, ALU.mult)
            link(dve.scalar_tensor_tensor(row_f[:, :, :], tile_f[:, :, :], -float(P), posf[:, :, :], ALU.mult, ALU.add))
            for k in range(TOPK):
                for t in range(NT):
                    dve.tensor_scalar(oh_row[:, NT * k + t, :], iota_n[:, 0:P], row_f[:, k, t:t + 1], None, ALU.is_equal)
                    dve.tensor_scalar(oh_tile[:, NT * k + t, :], iota_s[:, :], tile_f[:, k, t:t + 1], tok[:, t:t + 1],
                                      ALU.is_equal, ALU.mult).then_inc(place_ready, 1)
            dve.sem_inc(pos_ready, 1)
            dve.wait_ge(place_mm, 1)
            dve.tensor_copy(slot_sb[:, :], ps[:, 7, 256:256 + SLOTS + 1]).then_inc(slots_ready, 1)
            dve.wait_ge(we_ready, 1)
            link(dve.tensor_scalar(wdiff[:, :], wexp[:, :], 1.0, None, ALU.add))
            link(dve.reciprocal(wts[:, 0, :], wdiff[:, :]))
            link(dve.tensor_tensor(wts[:, 1, :], wts[:, 0, :], wexp[:, :], ALU.mult))
            for c in range(KD, NC):
                econv_dve(dve, 0, 0, c, c % 4)

            s_reg = dve.alloc_register("dve_slot")
            dve.wait_ge(pos_ready, 1)
            for u in range(2):
                dve.wait_ge(x2_st[u], 16 * (NT // 2 + 1))
                dve.wait_ge(xf_st[u], 16 * (NT // 2 + 1))

            def xgt_low(s):
                for b in range(2):
                    dve.wait_ge(xgt_hi, 2 * s + b + 1)
                    dve.scalar_tensor_tensor(xgt[1][:, 4 * b:4 * b + 4, :], ps[:, b, :].rearrange("p (k n) -> p k n", k=4), F_UP,
                                             xgt[0][:, 4 * b:4 * b + 4, :], ALU.mult, ALU.subtract).then_inc(xgt_done, 1)

            def hidt_low(s):
                dve.wait_ge(hidt_hi, s + 1)
                dve.tensor_tensor(hidt[1][:, :, :], ps[:, 6, :].rearrange("p (k n) -> p k n", k=KF), hidt[0][:, :, :],
                                  ALU.subtract).then_inc(hidt_done, 1)

            def y_out(s, slot):
                dve.wait_ge(g2_done, s + 1)
                dve.wait_ge(y_st, 16 * s + 16)
                dve.scalar_tensor_tensor(y_sb[:, :], banks(4, 2), 1.0 / (G_UP * W_UP), eb[slot][:, 2 * F:], ALU.mult, ALU.add).then_inc(y_ready, 1)

            def slot_dve(s, e, slot, other, convert, very_first=False):
                if not very_first:
                    hidt_low(s - 1)
                if convert:
                    for c in range(KD):
                        econv_dve(dve, e + 1, 1 - slot, c, c % 4)
                dve.wait_ge(g1_done, s + 1)
                for b, g in enumerate((ga, gb)):
                    dve.scalar_tensor_tensor(g[:, :], ps[:, 2 + b, :], 1.0 / (F_UP * W_UP), eb[slot][:, b * F:(b + 1) * F],
                                             ALU.mult, ALU.add).then_inc(ab_done, 1)
                dve.wait_ge(silu_done, s + 1)
                dve.wait_ge(ab_done, 2 * s + 2)
                dve.scalar_tensor_tensor(hid[:, :], ga[:, :], G_UP, gb[:, :], ALU.mult, ALU.mult).then_inc(hid_ready, 1)
                xgt_low(s + 1)
                if not very_first:
                    y_out(s - 1, other)
                if convert:
                    for c in range(KD, NC):
                        econv_dve(dve, e + 1, 1 - slot, c, c % 4)

            xgt_low(0)

            def expert_dve(e, slot, turn, first=False, last=False):
                n = dve.value_load(toti[0:1, 1, ds(e, 1)], min_val=1, max_val=NT)
                wait_alone(dve, eb_ld[slot], 48 * turn)
                if first:
                    slot_dve(0, e, slot, None, True, very_first=True)
                    dve.reg_mov(s_reg, 1)
                else:
                    slot_dve(dve.snap(s_reg, min_val=1, max_val=SLOTS - 1), e, slot, 1 - slot, not last)
                    dve.reg_add(s_reg, s_reg, 1)
                with dve.If(n > 1):
                    with dve.Fori(1, n):
                        slot_dve(dve.snap(s_reg, min_val=1, max_val=SLOTS - 1), e, slot, slot, False)
                        dve.reg_add(s_reg, s_reg, 1)

            expert_dve(0, 0, 1, first=True)
            expert_dve(1, 1, 1)
            with dve.Fori(1, NE // 2 - 1) as j:
                expert_dve(2 * j, 0, j + 1)
                expert_dve(2 * j + 1, 1, j + 1)
            expert_dve(NE - 2, 0, NE // 2)
            expert_dve(NE - 1, 1, NE // 2, last=True)
            s_end = dve.snap(s_reg, min_val=1, max_val=SLOTS)
            hidt_low(s_end - 1)
            y_out(s_end - 1, 1)

            dve.wait_ge(x2e_ld, 16)
            for q in range(TOPK * NT):
                t, k = q // TOPK, q % TOPK
                rows = LAST if t == NT - 1 else P
                dve.wait_ge(yg_ld[q % RING], 16 * (q // RING + 1))
                if k:
                    dve.wait_ge(y_added, q)
                dve.scalar_tensor_tensor(x2e[0:rows, t, :], yg[q % RING][0:rows, :], wts[0:rows, k, t:t + 1], x2e[0:rows, t, :],
                                         ALU.mult, ALU.add).then_inc(y_added, 1)


def kernel(**inputs):
    import numpy as np
    import concourse.bacc as bacc
    from concourse.bass_utils import run_bass_kernel_spmd

    g = {k: np.asarray(v) for k, v in inputs.items()}
    n, d = g["x"].shape
    nt = -(-n // P)
    e = g["src"].shape[0]
    et = -(-e // P)
    eg = -(-et // P)
    rows = np.concatenate([g["dst"], np.full(eg * P * P - e, n - 1, g["dst"].dtype)])
    et += UNIT - 1
    src = np.concatenate([g["src"], np.full(et * P - e, -1, g["src"].dtype)])
    dst = np.concatenate([g["dst"], np.full(et * P - e, n - 1, g["dst"].dtype)])
    arrays = {
        "x": np.concatenate([g["x"], np.zeros((nt * P - n, d), g["x"].dtype)]),
        "src_t": src.reshape(et, P).T,
        "dst_t": dst.reshape(et, P).T,
        "dst_rows": rows.reshape(eg, P, P).transpose(1, 0, 2),
        "W": g["L0_gnn_W"],
        "a": g["L0_gnn_a"].reshape(2, d),
        "wqkv": g["L0_mix_w_qkv"].T,
        "wproj": g["L0_mix_w_proj"].T,
        "bproj": g["L0_mix_b_proj"].reshape(1, d),
        "ln_w": g["L0_ffn_ln_w"].reshape(1, d),
        "Wg": g["L0_ffn_Wg"],
        "bg": g["L0_ffn_bg"].reshape(1, -1),
        "W1a": g["L0_ffn_W1a"], "b1a": g["L0_ffn_b1a"], "W1b": g["L0_ffn_W1b"], "b1b": g["L0_ffn_b1b"],
        "W2": g["L0_ffn_W2"], "b2": g["L0_ffn_b2"],
    }
    nc = bacc.Bacc("TRN2", target_bir_lowering=False, num_devices=1)
    feed, args = {}, []
    for name, array in arrays.items():
        array = np.ascontiguousarray(array)
        feed[f"in_{name}"] = array
        args.append(nc.dram_tensor(f"in_{name}", array.shape, mybir.dt.from_np(array.dtype), kind="ExternalInput").ap())
    args.append(nc.dram_tensor("out_0", (n, d), F32, kind="ExternalOutput").ap())
    build(nc, *args)
    result = run_bass_kernel_spmd(nc, [feed], core_ids=[0])
    return result.results[0]["out_0"]
```

```python
from contextlib import ExitStack

import concourse.bass as bass
from concourse import mybir

F32 = mybir.dt.float32
F16 = mybir.dt.float16
BF16 = mybir.dt.bfloat16
I32 = mybir.dt.int32
ALU = mybir.AluOpType
ACT = mybir.ActivationFunctionType
AX = mybir.AxisListType.X

P = 128
HALF = 512
UNIT = 5
DVE_TILES = 2
MIN_STEPS = 6
SLOPE = 0.1
EPS_LN = 1e-5
EPS_GNN = 1e-5
EPS_RMS = 1.1920928955078125e-07
X_UP, W_UP = 2.0 ** 10, 2.0 ** 10
H_UP = 2.0 ** 6
K_UP = Q_UP = 2.0 ** 10
C_UP = 4.0
M_UP = 2.0 ** 12
F_UP = 2.0 ** 8
G_UP = 2.0 ** 4
BIG = 1024.0


def ds(start, size):
    return bass.ds(start, size)


def build(nc, x, src_t, dst_t, dst_rows, W, a, wqkv, wproj, bproj, ln_w, Wg, bg, W1a, b1a, W1b, b1b, W2, b2, out):
    N, D = out.shape
    NT = x.shape[0] // P
    NP = NT * P
    LAST = N - (NT - 1) * P
    KD = D // P
    ET = src_t.shape[1]
    EG = dst_rows.shape[1]
    ER = ET - (UNIT - 1)
    NE, _, F = W1a.shape
    KF = F // P
    NPAIR = D // P
    TOPK = 2
    SLOTS = (TOPK * N + NE * (P - 1)) // P
    assert NT == 10 and KD == 8 and F == HALF and D == 2 * HALF and SLOTS == 27 and ER <= HALF

    x1_dram = nc.dram_tensor("x1_scratch", (NP, D), F32, kind="Internal").ap()
    x2_dram = nc.dram_tensor("x2_scratch", (NP, D), F32, kind="Internal").ap()
    xf_dram = nc.dram_tensor("xf_scratch", (NP, D), F32, kind="Internal").ap()
    y_dram = nc.dram_tensor("y_scratch", (SLOTS * P, D), F32, kind="Internal").ap()

    with ExitStack() as ctx:
        def sb(name, shape, dt):
            return ctx.enter_context(nc.sbuf_tensor(name, shape, dt))

        def sem(name):
            return ctx.enter_context(nc.semaphore(name))

        ident = sb("ident", [P, P], F32)
        iota_n = sb("iota_n", [P, NP], F16)
        tri = sb("tri", [P, P], BF16)
        ones_b = sb("ones_b", [P, P], BF16)
        ones_f = sb("ones_f", [P, P], F32)
        ones_h = sb("ones_h", [P, 2], F16)
        zero_h = sb("zero_h", [P, HALF], F16)
        eps_ln = sb("eps_ln", [P, 1], F32)
        eps_rms = sb("eps_rms", [P, 1], F32)
        src_f = sb("src_f", [P, ET], F32)
        dst_f = sb("dst_f", [P, ET], F32)
        dst_neg = sb("dst_neg", [P, ET], F32)
        bproj_b = sb("bproj_b", [P, D], F32)
        lnw_b = sb("lnw_b", [P, D], F32)
        wg_sb = sb("wg_sb", [P, KD, NE], F32)
        bg_b = sb("bg_b", [P, NE], F32)
        stats = sb("stats", [P, 2, 12], F32)
        mv = sb("mv", [P, 2, 2], F32)
        sd = sb("sd", [P, 2, 1], F32)
        rstd = sb("rstd", [P, 2, 1], F32)
        nbias = sb("nbias", [P, 2, 1], F32)
        al_part = sb("al_part", [P, 2, 2, NT], F32)
        al_ar = sb("al_ar", [P, 2, NT], F32)
        ar_slope = sb("ar_slope", [P, 2, NT], F32)
        ks = sb("ks", [P, KD], F32)
        rks = sb("rks", [P, KD], F32)
        kmax = sb("kmax", [P, 2, 2], F32)
        qred = sb("qred", [P, 2, 3, 8], F32)
        rsum = sb("rsum", [P, 2, 3], F32)
        urep = sb("urep", [P, 2, EG, 16], F32)
        ured = sb("ured", [P, 2, EG], F32)
        win = sb("win", [16, 8], F32)
        iota_w = sb("iota_w", [16, 2], F32)
        lohi = sb("lohi", [1, 32], I32)
        iota_e = sb("iota_e", [P, NE], F32)
        valid = sb("valid", [P, 1], F32)
        lg = sb("lg", [P, NE], F32)
        top8 = sb("top8", [P, 8], F32)
        idx8 = sb("idx8", [P, 8], mybir.dt.uint32)
        idxf = sb("idxf", [P, 8], F32)
        ssq = sb("ssq", [P, 3], F32)
        onehot = sb("onehot", [P, TOPK, NT, NE], F32)
        mask = sb("mask", [P, NT, NE], BF16)
        before = sb("before", [P, NT + 1, NE], BF16)
        wdiff = sb("wdiff", [P, NT], F32)
        wexp = sb("wexp", [P, NT], F32)
        wts = sb("wts", [P, TOPK, NT], F32)
        rank = sb("rank", [P, NT, NE], F32)
        ranked = sb("ranked", [P, NT, NE], F32)
        tot = sb("tot", [P, 6, NE], F32)
        toti = sb("toti", [P, 3, NE], I32)
        posf = sb("posf", [P, TOPK, NT], F32)
        pos = sb("pos", [P, TOPK, NT], I32)
        tok = sb("tok", [P, NT], F32)
        iota_s = sb("iota_s", [P, SLOTS + 1], F32)
        tile_i = sb("tile_i", [P, TOPK, NT], I32)
        tile_f = sb("tile_f", [P, TOPK, NT], F32)
        row_f = sb("row_f", [P, TOPK, NT], F32)
        slot_sb = sb("slot_sb", [P, SLOTS + 1], I32)

        base = (nc.sbuf_base + 63) // 64 * 64
        ctx.enter_context(nc.sbuf_tensor("arena", [P, (nc.sbuf_usable_end - 64 - base) // 64 * 16 - 32], F32))
        KB = 1024
        assert base + 184 * KB <= nc.sbuf_usable_end

        def at(name, kb, shape, dt):
            return nc.alloc_sbuf_tensor_at(name, shape, dt, offset=base + int(kb * KB))

        xt = [at(f"xt{p}", 20 * p, [P, KD, NP], F16) for p in range(2)]
        h = [at(f"h{p}", 40 + 20 * p, [P, NT, D], F16) for p in range(2)]
        adj = [at(f"adj{p}", 80 + 25.5 * p, [P, NT, NP], F16) for p in range(2)]
        w_sb = [[at(f"w{s}{p}", 132 + 16 * s + 8 * p, [P, KD, HALF], F16) for p in range(2)] for s in range(2)]
        stage = [at(f"stage{s}", 164 + 2 * s, [P, HALF], F32) for s in range(2)]
        stage_h = at("stage_h", 40, [P, KD, HALF], F32)
        x_in = [at(f"x_in{u}", 80 + 4 * u, [P, D], F32) for u in range(2)]
        x_n = [at(f"x_n{u}", 88 + 4 * u, [P, D], F32) for u in range(2)]
        a_b = at("a_b", 96, [P, 2, D], F32)
        junk = [at(f"junk{q}", 104 + 2 * q, [P, HALF], F32) for q in range(2)]
        idx_in = at("idx_in", 120, [P, 2, ET], I32)
        rows_i = at("rows_i", 108, [P, EG, P], I32)
        rows_f = at("rows_f", 110, [P, EG, P], F32)
        rtile = at("rtile", 112, [16, 4, ER], F32)
        iota_u = at("iota_u", 118, [16, ER], F32)
        oh_src = [at(f"oh_src{u}", 148 + 2.5 * u, [P, NP], F16) for u in range(UNIT)]
        al_rep = at("al_rep", 170.5, [P, NT, P], F32)
        al_row = at("al_row", 160.5, [P, NP], F32)
        edge = [at(f"edge{u}", 165.5 + 5 * u, [P, NP], F32) for u in range(2)]
        slope = at("slope", 175.5, [P, NP], F32)
        oh_dst = [at(f"oh_dst{u}", 180.5 + 0.25 * u, [P, P], F16) for u in range(DVE_TILES)]
        oh_dst_act = at("oh_dst_act", 181, [P, 2 * (UNIT - DVE_TILES), P], F16)
        apart = at("apart", 182.5, [P, UNIT - DVE_TILES, P], F32)
        x1 = [at(f"x1{u}", 168 + 4 * u, [P, D], F32) for u in range(2)]
        neg = at("neg", 176, [P, D], F32)
        poz = at("poz", 180, [P, D], F32)
        kv = [[at(f"kv{m}{p}", 40 + 20 * m + 10 * p, [P, NT, HALF], F16) for p in range(2)] for m in range(2)]
        k_exp = [at(f"k_exp{u}", 80 + 5 * u, [P, NP], F32) for u in range(2)]
        ctxt = [at(f"ctxt{p}", 90 + 2 * p, [P, NPAIR, P], F16) for p in range(2)]
        qt = [at(f"qt{p}", 40 + 20 * p, [P, KD, NP], F16) for p in range(2)]
        q_s = [at(f"q_s{u}", 168 + 2 * u, [P, HALF], F32) for u in range(2)]
        w_proj = [w_sb[0], [at(f"w_proj{p}", (172, 80)[p], [P, KD, HALF], F16) for p in range(2)]]
        m_sb = [at(f"m{p}", 94 + 16 * p, [P, KD, D], F16) for p in range(2)]
        x1m = [at(f"x1m{u}", 4 * u, [P, D], F32) for u in range(2)]
        x2m = [at(f"x2m{u}", 8 + 4 * u, [P, D], F32) for u in range(2)]
        xfm = [at(f"xfm{u}", 16 + 4 * u, [P, D], F32) for u in range(2)]
        oh_row = at("oh_row", 88, [P, TOPK * NT, P], F16)
        oh_tile = at("oh_tile", 126, [P, TOPK * NT, SLOTS + 1], F16)
        xft = at("xft", 24, [P, KD, P], F32)
        sqj = at("sqj", 28, [P, D], F32)
        ew = [[at(f"ew{s}{p}", (136, 88)[s] + 24 * p, [P, KD + KF, D], F16) for p in range(2)] for s in range(2)]
        est = [at(f"est{s}", (80, 84, 32, 36)[s], [P, D], F32) for s in range(4)]
        xg = at("xg", 0, [P, D], F32)
        xg_second = at("xg_second", 28, [P, D], F32)
        xgt = [at(f"xgt{p}", 4 + 2 * p, [P, KD, P], F16) for p in range(2)]
        ga = at("ga", 8, [P, HALF], F32)
        gb = at("gb", 10, [P, HALF], F32)
        hid = at("hid", 12, [P, HALF], F32)
        hidt = [at(f"hidt{p}", 14 + p, [P, KF, P], F16) for p in range(2)]
        y_sb = at("y_sb", 16, [P, D], F32)
        eb = [at(f"eb{s}", 20 + 20 * s, [P, 2 * D], F32) for s in range(2)]
        RING = 8
        yg = [at(f"yg{q}", 48 + 4 * q, [P, D], F32) for q in range(RING)]
        x2e = at("x2e", 136, [P, NT, D], F32)

        ps = ctx.enter_context(nc.psum_tensor("ps", [P, 8, HALF], F32))

        def banks(b, n):
            return ps[:, b:b + n, :].rearrange("p b n -> p (b n)")

        const_set = sem("const_set"); const_ld = sem("const_ld"); a_ld = sem("a_ld"); dve_c = sem("dve_c")
        idx_ready = sem("idx_ready"); win_mm = sem("win_mm"); win_ready = sem("win_ready")
        stage_ld = [sem(f"stage_ld{s}") for s in range(2)]; wh_ld = [sem(f"wh_ld{g}") for g in range(KD // 2)]
        w_hi = sem("w_hi"); w_done = sem("w_done");
        xin_ld = [sem(f"xin_ld{u}") for u in range(2)]
        ln_mv = sem("ln_mv"); ln_sd = sem("ln_sd"); ln_nb = sem("ln_nb"); xn_ready = sem("xn_ready")
        xn_turned = sem("xn_turned"); xt_hi = sem("xt_hi"); xt_done = sem("xt_done")
        g_done = sem("g_done"); g_hi = sem("g_hi"); g_free = sem("g_free")
        dve_ln = sem("dve_ln")
        alrep_ready = sem("alrep_ready"); alrow_mm = sem("alrow_mm"); alrow_ready = sem("alrow_ready")
        oh_ready = sem("oh_ready");  oh_free = sem("oh_free"); apart_ready = sem("apart_ready"); oh_act_ready = sem("oh_act_ready"); win_done = sem("win_done")
        z_ready = sem("z_ready"); lr_ready = sem("lr_ready"); e_ready = sem("e_ready")
        cnt_ready = sem("cnt_ready"); adj_hi = sem("adj_hi"); adj_done = sem("adj_done")
        gnn_done = sem("gnn_done"); gnn_free = sem("gnn_free"); neg_ready = sem("neg_ready"); neg_exp = sem("neg_exp")
        dve_g = sem("dve_g"); x1_ready = sem("x1_ready")
        x1_ld = [sem(f"x1_ld{u}") for u in range(2)]; x1_st = [sem(f"x1_st{u}") for u in range(2)]
        k_done = sem("k_done"); km_ready = sem("km_ready"); ke_ready = sem("ke_ready"); dve_k = sem("dve_k")
        kt_mm = sem("kt_mm"); kt_hi = sem("kt_hi"); kt_done = sem("kt_done"); ke_zero = sem("ke_zero")
        ctx_mm = sem("ctx_mm"); ctx_hi = sem("ctx_hi"); ctx_done = sem("ctx_done")
        q_exp = sem("q_exp"); q_norm = sem("q_norm"); q_mm = sem("q_mm"); q_hi = sem("q_hi"); qt_done = sem("qt_done")
        dve_q = sem("dve_q")
        rks_ready = sem("rks_ready"); m_mm = sem("m_mm"); m_hi = sem("m_hi"); m_done = sem("m_done")
        mix_done = sem("mix_done"); x2_ready = sem("x2_ready"); ln2_mv = sem("ln2_mv"); ln2_sd = sem("ln2_sd"); ln2_nb = sem("ln2_nb")
        act_m = sem("act_m"); rms_sd = sem("rms_sd"); xf_ready = sem("xf_ready"); xf_mm = sem("xf_mm"); xft_ready = sem("xft_ready")
        lg_mm = sem("lg_mm"); lg_ready = sem("lg_ready"); dve_m = sem("dve_m"); dve_x = sem("dve_x"); wd_ready = sem("wd_ready"); we_ready = sem("we_ready")
        x1m_ld = [sem(f"x1m_ld{u}") for u in range(2)]; x2_st = [sem(f"x2_st{u}") for u in range(2)]; xf_st = [sem(f"xf_st{u}") for u in range(2)]
        mask_ready = sem("mask_ready"); rank_mm = sem("rank_mm"); dve_r = sem("dve_r"); pos_ready = sem("pos_ready")
        place_ready = sem("place_ready"); place_mm = sem("place_mm"); slots_ready = sem("slots_ready")
        est_ld = [sem(f"est_ld{s}") for s in range(4)]
        ew_hi = sem("ew_hi"); ew_done = sem("ew_done"); eb_ld = [sem(f"eb_ld{s}") for s in range(2)]
        xg_ld = sem("xg_ld"); xg_second_ld = sem("xg_second_ld"); xg_mm = sem("xg_mm"); xgt_hi = sem("xgt_hi"); xgt_done = sem("xgt_done")
        g1_done = sem("g1_done"); ab_done = sem("ab_done"); silu_done = sem("silu_done"); hid_ready = sem("hid_ready")
        hid_mm = sem("hid_mm"); hidt_hi = sem("hidt_hi"); hidt_done = sem("hidt_done"); g2_done = sem("g2_done"); y_ready = sem("y_ready"); y_st = sem("y_st"); y_fill = sem("y_fill")
        yg_ld = [sem(f"yg_ld{q}") for q in range(RING)]; x2e_ld = sem("x2e_ld")
        y_added = sem("y_added"); o_st = sem("o_st")

        halves = [W[:, 0:HALF], W[:, HALF:D]]
        for i in range(2):
            halves.append(wqkv[:, D + i * HALF:D + (i + 1) * HALF])
            halves.append(wqkv[:, 2 * D + i * HALF:2 * D + (i + 1) * HALF])
        halves += [wqkv[:, i * HALF:(i + 1) * HALF] for i in range(2)]
        J_K, J_V, J_Q, J_P = (2, 4), (3, 5), 6, 8
        BANK = {0: 4, 1: 4, 3: 0, 5: 3, 6: 3, 7: 3}
        G_BASE = {0: 0, 1: 10, 3: 20, 5: 30, 6: 40, 7: 50}

        def tiles(e, body, peel=1):
            body(0, 0, None, 0)
            with e.Fori(0, (NT - 1 - peel) // 2) as i:
                body(2 * i + 1, 1, i, 0)
                body(2 * i + 2, 0, i, 1)
            for t in range(NT - peel, NT - 1):
                body(t, t % 2, (t - 1) // 2, (t - 1) % 2)
            body(NT - 1, 1, None, 0)

        def turns(t, u, i, s):
            return (t // 2 + 1) if isinstance(t, int) else (i + 1 if s == 0 else i + 2)

        def split_mm(pe, outs, lhs, rhs, first, last, done=None):
            mm = None
            for n, o in enumerate(outs):
                pe.matmul(o, lhs[0], rhs[n][0], start=first, stop=False, skip_group_check=True)
                pe.matmul(o, lhs[0], rhs[n][1], start=False, stop=False, skip_group_check=True)
            for n, o in enumerate(outs):
                mm = pe.matmul(o, lhs[1], rhs[n][0], start=False, stop=last, skip_group_check=True)
            return mm

        def conv_act(act, j, i, u):
            act.wait_ge(stage_ld[u], 16 * (KD // 2 * (j - 1) + i + 1))
            if j - 2 in J_K:
                act.wait_ge(k_done, 4 * J_K.index(j - 2) + 4)
            elif j >= 2:
                act.wait_ge(g_done, G_BASE[j - 2] + NT)
            act.activation(w_sb[j % 2][0][:, ds(2 * i + u, 1), :], stage[u][:, :], ACT.Copy, scale=W_UP).then_inc(w_hi, 1)

        def conv_dve(dve, j, i, u):
            dve.wait_ge(w_hi, KD * j + 2 * i + u + 1)
            dve.scalar_tensor_tensor(w_sb[j % 2][1][:, ds(2 * i + u, 1), :], stage[u][:, :], W_UP,
                                     w_sb[j % 2][0][:, ds(2 * i + u, 1), :], ALU.mult, ALU.subtract).then_inc(w_done, 1)

        def pconv_act(act, c, u):
            act.wait_ge(stage_ld[u], 16 * (KD // 2 * (J_P - 1) + c + 1))
            act.wait_ge(g_done, G_BASE[J_Q] + NT)
            act.activation(w_proj[u][0][:, ds(c, 1), :], stage[u][:, :], ACT.Copy, scale=W_UP).then_inc(w_hi, 1)

        def pconv_dve(dve, c, u):
            dve.wait_ge(w_hi, KD * J_P + 2 * c + u + 1)
            dve.scalar_tensor_tensor(w_proj[u][1][:, ds(c, 1), :], stage[u][:, :], W_UP, w_proj[u][0][:, ds(c, 1), :],
                                     ALU.mult, ALU.subtract).then_inc(w_done, 1)

        def fconv_act(act, i, s):
            act.wait_ge(est_ld[s], 32 * (i + 1))
            act.activation(ew[0][0][:, ds(2 * i + s, 1), :], est[s][:, :], ACT.Copy, scale=W_UP).then_inc(ew_hi, 1)

        def fconv_dve(dve, i, s):
            dve.wait_ge(ew_hi, 2 * i + s + 1)
            dve.scalar_tensor_tensor(ew[0][1][:, ds(2 * i + s, 1), :], est[s][:, :], W_UP, ew[0][0][:, ds(2 * i + s, 1), :],
                                     ALU.mult, ALU.subtract).then_inc(ew_done, 1)

        def econv_act(act, e, slot, c, s):
            act.wait_ge(est_ld[s], 32 * (NC // 4 * e + c // 4 + 1 + (KD // 4 if s < 2 else -(KD // 4))))
            act.activation(ew[slot][0][:, c, :], est[s][:, :], ACT.Copy, scale=W_UP).then_inc(ew_hi, 1)

        def econv_dve(dve, e, slot, c, s):
            dve.wait_ge(ew_hi, (KD + KF) * e + c + 1)
            dve.scalar_tensor_tensor(ew[slot][1][:, c, :], est[s][:, :], W_UP, ew[slot][0][:, c, :],
                                     ALU.mult, ALU.subtract).then_inc(ew_done, 1)

        NC = KD + KF
        EARLY = 6

        def wait_alone(e, s, value):
            if not isinstance(value, int):
                value = e.to_reg(value)
                e.wait_ge(const_set, 19)
            e.wait_ge(s, value)

        block = ctx.enter_context(nc.Block())

        @block.sync
        def _(sp):
            sp.dma_start(x_in[0][:, :], x[0:P, :]).then_inc(xin_ld[0], 16)
            sp.dma_start(x_in[1][:, :], x[P:2 * P, :]).then_inc(xin_ld[1], 16)
            for g in range(KD // 2):
                sp.dma_start(stage_h[:, 2 * g:2 * g + 2, :],
                             halves[0][2 * g * P:(2 * g + 2) * P, :].rearrange("(k p) n -> p k n", p=P)).then_inc(wh_ld[g], 16)
            for q in range(2):
                sp.dma_start(a_b[:, q, :], a[q:q + 1, :].to_broadcast([P, D])).then_inc(a_ld, 16)

            def load_chunk(j, i, u):
                sp.wait_ge(w_done, KD * j + 2 * i + u + 1)
                sp.dma_start(stage[u][:, :], halves[j][ds((2 * i + u) * P, P), :]).then_inc(stage_ld[u], 16)

            def load_half(j):
                with sp.Fori(0, KD // 2) as i:
                    for u in range(2):
                        load_chunk(j, i, u)

            def load_pair(i):
                for u in range(2):
                    sp.wait_ge(xn_ready, 2 * i + u + 1)
                    sp.dma_start(x_in[u][:, :], x[ds((2 * i + u + 2) * P, P), :]).then_inc(xin_ld[u], 16)
                    load_chunk(1, i, u)

            load_pair(0)
            for t_, s_ in ((idx_in[:, 0, :], src_t), (idx_in[:, 1, :], dst_t), (rows_i[:, :, :], dst_rows),
                           (bproj_b[:, :], bproj.to_broadcast([P, D])), (lnw_b[:, :], ln_w.to_broadcast([P, D])),
                           (wg_sb[:, :, :], Wg.rearrange("(k p) e -> p k e", p=P)), (bg_b[:, :], bg.to_broadcast([P, NE]))):
                sp.dma_start(t_, s_).then_inc(const_ld, 16)
            with sp.Fori(1, KD // 2) as i:
                load_pair(i)
            load_half(2)
            for u in range(2):
                if u == 0:
                    sp.wait_ge(adj_done, NT + 2)
                sp.dma_start(x1[u][:, :], x[u * P:(u + 1) * P, :]).then_inc(x1_ld[u], 16)

            def gnn_io(t, u, n, load):
                sp.wait_ge(x1_ready, t + 1)
                sp.dma_start(x1_dram[ds(t * P, P), :], x1[u][:, :]).then_inc(x1_st[u], 16)
                if load:
                    sp.wait_ge(x1_st[u], 16 * n)
                    sp.dma_start(x1[u][:, :], x[ds((t + 2) * P, P), :]).then_inc(x1_ld[u], 16)

            with sp.Fori(0, NT // 2 - 1) as i:
                for u in range(2):
                    gnn_io(2 * i + u, u, i + 1, True)
            for u in range(2):
                gnn_io(NT - 2 + u, u, NT // 2, False)
            for j in range(3, J_P):
                load_half(j)
            with sp.Fori(0, KD) as c:
                for u in range(2):
                    sp.wait_ge(w_done, KD * J_P + 2 * c + u + 1)
                    sp.dma_start(stage[u][:, :], wproj[ds(c * P, P), u * HALF:(u + 1) * HALF]).then_inc(stage_ld[u], 16)

            sp.sem_inc(ew_done, 4)
            for u in range(2):
                sp.sem_inc(x2_st[u], 16)
                sp.sem_inc(xf_st[u], 16)
            sp.sem_inc(y_st, 16)

            def load_expert(e, slot, bias_wait):
                for c in range(NC):
                    s = c % 4
                    sp.wait_ge(ew_done, NC * e + c + 1)
                    if c < KD:
                        sp.dma_start(est[s][:, 0:HALF], W1a[ds(e, 1), c * P:(c + 1) * P, :]).then_inc(est_ld[s], 16)
                        sp.dma_start(est[s][:, HALF:D], W1b[ds(e, 1), c * P:(c + 1) * P, :]).then_inc(est_ld[s], 16)
                    else:
                        sp.dma_start(est[s][:, :], W2[ds(e, 1), (c - KD) * P:(c - KD + 1) * P, :]).then_inc(est_ld[s], 32)
                if bias_wait:
                    sp.wait_ge(ew_done, 4 + NC * e + KD + 1)
                sp.dma_start(eb[slot][:, 0:F], b1a[ds(e, 1), :].to_broadcast([P, F])).then_inc(eb_ld[slot], 16)
                sp.dma_start(eb[slot][:, F:2 * F], b1b[ds(e, 1), :].to_broadcast([P, F])).then_inc(eb_ld[slot], 16)
                sp.dma_start(eb[slot][:, 2 * F:], b2[ds(e, 1), :].to_broadcast([P, D])).then_inc(eb_ld[slot], 16)

            def mix_io(t, u, n, load):
                if load:
                    sp.wait_ge(x2_ready, t + 3)
                    sp.dma_start(x1m[u][:, :], x1_dram[ds((t + 2) * P, P), :]).then_inc(x1m_ld[u], 16)
                else:
                    sp.wait_ge(x2_ready, t + 3)
                sp.dma_start(x2_dram[ds(t * P, P), :], x2m[u][:, :]).then_inc(x2_st[u], 16)
                sp.wait_ge(xf_ready, t + 1)
                sp.dma_start(xf_dram[ds(t * P, P), :], xfm[u][:, :]).then_inc(xf_st[u], 16)

            sp.wait_ge(g_done, G_BASE[J_Q + 1] + NT)
            for u in range(2):
                sp.wait_ge(x1_st[u], 16 * NT // 2)
            for u in range(2):
                sp.dma_start(x1m[u][:, :], x1_dram[u * P:(u + 1) * P, :]).then_inc(x1m_ld[u], 16)
            def load_first(c, s):
                sp.wait_ge(ew_done, c + 3)
                sp.dma_start(est[s][:, 0:HALF], W1a[0:1, ds(c * P, P), :]).then_inc(est_ld[s], 16)
                sp.dma_start(est[s][:, HALF:D], W1b[0:1, ds(c * P, P), :]).then_inc(est_ld[s], 16)

            sp.wait_ge(m_done, 2 * KD + 2)
            with sp.Fori(0, NT // 2 - 1) as i:
                for u in range(2):
                    load_first(2 * i + u, u)
                    mix_io(2 * i + u, u, i + 1, True)
            for u in range(2):
                mix_io(NT - 2 + u, u, NT // 2, False)
            for c in range(KD, NC):
                sp.wait_ge(ew_done, c + 3)
                sp.dma_start(est[c % 4][:, :], W2[0:1, (c - KD) * P:(c - KD + 1) * P, :]).then_inc(est_ld[c % 4], 32)
            for u in range(2):
                sp.wait_ge(x2_st[u], 16 * (NT // 2 + 1))
                sp.wait_ge(xf_st[u], 16 * (NT // 2 + 1))
            sp.wait_ge(lg_ready, NT)
            sp.dma_start(eb[0][:, 0:F], b1a[0:1, :].to_broadcast([P, F])).then_inc(eb_ld[0], 16)
            sp.dma_start(eb[0][:, F:2 * F], b1b[0:1, :].to_broadcast([P, F])).then_inc(eb_ld[0], 16)
            sp.dma_start(eb[0][:, 2 * F:], b2[0:1, :].to_broadcast([P, D])).then_inc(eb_ld[0], 16)
            load_expert(1, 1, False)
            with sp.Fori(1, NE // 2) as j:
                load_expert(2 * j, 0, True)
                load_expert(2 * j + 1, 1, True)
            before_last = sp.value_load(toti[0:1, 2, NE - 2:NE - 1], min_val=NE - 1, max_val=SLOTS - 1)
            wait_alone(sp, g2_done, before_last)
            sp.dma_start(x2e[:, :, :], x2_dram.rearrange("(t p) d -> p t d", p=P)).then_inc(x2e_ld, 16)
            with sp.Fori(0, NT - 1) as t:
                sp.wait_ge(y_added, 2 * t + 2)
                sp.dma_start(out[ds(t * P, P), :], x2e[:, ds(t, 1), :]).then_inc(o_st, 16)
            sp.wait_ge(y_added, 2 * NT)
            sp.dma_start(out[(NT - 1) * P:N, :], x2e[0:LAST, NT - 1, :]).then_inc(o_st, 16)
            sp.wait_ge(o_st, 16 * NT)

        @block.gpsimd
        def _(pool):
            pool.memset(eps_ln[:, :], EPS_LN).then_inc(const_set, 1)
            pool.memset(ident[:, :], 0.0).then_inc(const_set, 1)
            pool.memset(tri[:, :], 0.0).then_inc(const_set, 1)
            pool.memset(valid[:, :], 1.0).then_inc(const_set, 1)
            pool.wait_ge(const_set, 4)
            pool.affine_select(out=ident[:, :], in_=ident[:, :], compare_op=ALU.not_equal, fill=1.0, base=0,
                               pattern=[[-1, P]], channel_multiplier=1).then_inc(const_set, 1)
            pool.affine_select(out=tri[:, :], in_=tri[:, :], compare_op=ALU.is_ge, fill=1.0, base=0,
                               pattern=[[-1, P]], channel_multiplier=1).then_inc(const_set, 1)
            pool.affine_select(out=valid[:, :], in_=valid[:, :], compare_op=ALU.is_ge, fill=0.0, base=LAST - 1,
                               pattern=[[0, 1]], channel_multiplier=-1).then_inc(const_set, 1)
            for t_, pattern, b_, mult in ((iota_n, [[1, NP]], 0, 0), (iota_w, [[P, 2]], 0, P), (iota_u, [[1, ER]], 0, 0),
                                          (iota_e, [[1, NE]], 0, 0), (tok, [[P, NT]], 0, 1),
                                          (iota_s, [[1, SLOTS + 1]], 0, 0)):
                pool.iota(t_[:, :], pattern, base=b_, channel_multiplier=mult,
                          allow_small_or_imprecise_dtypes=True).then_inc(const_set, 1)
            pool.memset(ones_b[:, :], 1.0).then_inc(const_set, 1)
            pool.memset(ones_f[:, :], 1.0).then_inc(const_set, 1)
            pool.memset(ones_h[:, :], 1.0).then_inc(const_set, 1)
            pool.memset(zero_h[:, :], 0.0).then_inc(const_set, 1)
            pool.memset(eps_rms[:, :], EPS_RMS).then_inc(const_set, 1)
            pool.memset(before[:, 0, :], 0.0).then_inc(const_set, 1)
            def adj_high(w, wu):
                pool.wait_ge(cnt_ready, w + 3)
                pool.tensor_copy(adj[0][:, ds(w, 1), :], edge[wu][:, :]).then_inc(adj_hi, 1)

            def window_pool(w, wu, i, s_):
                if not (isinstance(w, int) and w == 0):
                    adj_high(w - 1, 1 - wu)
                pool.wait_ge(z_ready, 2 * w + 2)
                pool.tensor_tensor(edge[wu][:, :], edge[wu][:, :], slope[:, :], ALU.add).then_inc(lr_ready, 1)

            tiles(pool, window_pool)
            adj_high(NT - 1, 1)
            pool.wait_ge(adj_done, NT + 2)
            pool.wait_ge(x1_ready, NT)
            for u in range(2):
                pool.memset(k_exp[u][:, N:NP], 0.0).then_inc(ke_zero, 1)
            for p_ in range(2):
                pool.memset(ctxt[p_][:, :, :], 0.0).then_inc(ke_zero, 1)

            pool.wait_ge(slots_ready, 1)
            for u in range(2):
                pool.wait_ge(xf_st[u], 16 * (NT // 2 + 1))
                pool.wait_ge(x2_st[u], 16 * (NT // 2 + 1))
            used = pool.value_load(toti[0:1, 2, NE - 1:NE], min_val=NE, max_val=SLOTS)

            def gather(s):
                if s > 1:
                    pool.wait_ge(xg_mm, 2 if s == 2 else 2 * s)
                pool.indirect_dma_start(out=(xg_second if s == 1 else xg)[:, :], out_offset=None, in_=xf_dram,
                                        in_offset=bass.IndirectOffsetOnAxis(ap=slot_sb[:, s:s + 1], axis=0)).then_inc(xg_second_ld if s == 1 else xg_ld, 16)

            for s in range(SLOTS + 1):
                if s <= NE:
                    gather(s)
                else:
                    with pool.If(used >= s):
                        gather(s)
            zeros = zero_h[:, :].bitcast(F32)
            fills = pool.alloc_register("pool_fills")
            pool.reg_mov(fills, 1)
            with pool.If(used < SLOTS):
                with pool.Fori(used, SLOTS) as s:
                    pool.dma_start(y_dram[ds(s * P, P), :].rearrange("p (r n) -> p r n", n=HALF // 2),
                                   zeros.unsqueeze(1).to_broadcast([P, 2 * D // HALF, HALF // 2])).then_inc(y_fill, 16)
                    pool.wait_ge(y_fill, 16 * pool.snap(fills, min_val=1, max_val=SLOTS))
                    pool.reg_add(fills, fills, 1)
            wait_alone(pool, y_st, 16 * used + 16)
            for q in range(TOPK * NT):
                t, k = q // TOPK, q % TOPK
                rows = LAST if t == NT - 1 else P
                if q >= RING:
                    pool.wait_ge(y_added, q - RING + 1)
                pool.indirect_dma_start(out=yg[q % RING][0:rows, :], out_offset=None, in_=y_dram,
                                        in_offset=bass.IndirectOffsetOnAxis(ap=pos[0:rows, k, t:t + 1], axis=0)).then_inc(yg_ld[q % RING], 16)

        @block.scalar
        def _(act):
            act.wait_ge(const_set, 1)
            act.sem_inc(xn_turned, 4)
            act.sem_inc(xf_mm, 4)

            def ln_deviation(t, u):
                act.wait_ge(ln_mv, t + 1)
                act.activation(sd[:, u, :], mv[:, u, 1:2], ACT.Sqrt, bias=eps_ln[:, 0:1]).then_inc(ln_sd, 1)

            def ln_norm(t, u):
                act.wait_ge(ln_nb, t + 1)
                act.wait_ge(xn_turned, 2 * t + 2)
                act.activation(x_n[u][:, :], x_in[u][:, :], ACT.Identity, bias=nbias[:, u, :], scale=rstd[:, u, :]).then_inc(xn_ready, 1)

            def xt_high(t, u):
                for b in range(2):
                    act.wait_ge(xn_turned, 2 * t + b + 5)
                    act.activation(xt[0][:, 4 * b:4 * b + 4, ds(t * P, P)], ps[:, 2 * u + b, :].rearrange("p (k n) -> p k n", k=4),
                                   ACT.Copy, scale=X_UP).then_inc(xt_hi, 1)

            def h_high(half):
                def body(t, u, i, s):
                    if half == 0 and not (isinstance(t, int) and t > NT - 2):
                        xt_high(t + 1, 1 - u)
                    if half == 0 and not (isinstance(t, int) and t > NT - 3):
                        ln_deviation(t + 2, u)
                        ln_norm(t + 2, u)
                    if i is not None:
                        conv_act(act, half + 1, i, s)
                    act.wait_ge(g_done, G_BASE[half] + t + 1)
                    act.activation(h[0][:, ds(t, 1), half * HALF:(half + 1) * HALF], ps[:, 4 + u, :], ACT.Copy,
                                   scale=H_UP / (X_UP * W_UP)).then_inc(g_hi, 1)
                return body

            ln_deviation(0, 0)
            ln_norm(0, 0)
            for g in range(KD // 2):
                act.wait_ge(wh_ld[g], 16)
                act.activation(w_sb[0][0][:, 2 * g:2 * g + 2, :], stage_h[:, 2 * g:2 * g + 2, :], ACT.Copy, scale=W_UP).then_inc(w_hi, 2)
                if g == 0:
                    ln_deviation(1, 1)
                    ln_norm(1, 1)
                    xt_high(0, 0)
            tiles(act, h_high(0), 3)
            tiles(act, h_high(1))
            for b, bank, n in ((0, 6, HALF), (1, 7, HALF), (2, 4, NP - 2 * HALF)):
                act.wait_ge(alrow_mm, 1)
                ins = act.activation(al_row[:, b * HALF:b * HALF + n], ps[:, bank, 0:n], ACT.Copy)
            ins.then_inc(alrow_ready, 1)
            act.wait_ge(alrow_ready, 1)

            steps_r = act.alloc_register("act_steps")
            act.reg_mov(steps_r, 0)
            tile_r = act.alloc_register("act_tile")
            act.wait_ge(win_ready, 2)

            def one_hots_act(w):
                first = act.snap(tile_r, min_val=0, max_val=ET - UNIT)
                n_u = act.snap(steps_r, min_val=0, max_val=NT * ER)
                n = UNIT - DVE_TILES
                for u in range(n):
                    act.activation(apart[:, u, :], iota_n[:, ds(w * P, P)], ACT.Square,
                                   bias=dst_neg[:, ds(first + DVE_TILES + u, 1)]).then_inc(apart_ready, 1)
                act.wait_ge(apart_ready, n * n_u + n)
                act.wait_ge(oh_free, UNIT * n_u + UNIT)
                act.activation(oh_dst_act[:, ds((n_u % 2) * n, n), :], apart[:, :, :], ACT.Relu,
                               bias=ones_f[:, 0:1], scale=-2.0).then_inc(oh_act_ready, 1)
                act.wait_ge(oh_act_ready, n_u + 1)
                act.reg_add(steps_r, steps_r, 1)
                act.reg_add(tile_r, tile_r, UNIT)

            def window_act(w, wu, i, s_):
                lo = act.value_load(lohi[0:1, ds(w, 1)], min_val=0, max_val=ER - 1)
                steps = act.value_load(lohi[0:1, ds(16 + w, 1)], min_val=MIN_STEPS, max_val=ER)
                act.reg_mov(tile_r, lo)
                one_hots_act(w)
                act.wait_ge(adj_done, w + 1)
                act.activation(edge[wu][:, :], al_row[:, :], ACT.Identity, bias=ar_slope[:, 0, ds(w, 1)], scale=SLOPE).then_inc(z_ready, 1)
                one_hots_act(w)
                act.activation(slope[:, :], al_row[:, :], ACT.Relu, bias=ar_slope[:, 1, ds(w, 1)], scale=1.0 - SLOPE).then_inc(z_ready, 1)
                for _ in range(3):
                    one_hots_act(w)
                act.wait_ge(lr_ready, w + 1)
                act.activation(edge[wu][:, :], edge[wu][:, :], ACT.Exp, scale=-1.0).then_inc(e_ready, 1)
                with act.Fori(MIN_STEPS - 1, steps):
                    one_hots_act(w)

            tiles(act, window_act)

            def gnn_exp(t, u, i, s):
                act.wait_ge(neg_ready, t + 1)
                act.activation(neg[:, :], neg[:, :], ACT.Exp).then_inc(neg_exp, 1)

            act.wait_ge(const_set, 19)
            with act.Fori(0, NT) as t:
                gnn_exp(t, 0, None, 0)

            for kh in range(2):
                def k_turn(c):
                    for b, n in enumerate((4, 4, 2)):
                        q = 12 * kh + 3 * c + b
                        act.wait_ge(kt_mm, q + 1)
                        act.activation(kv[0][0][:, 4 * b:4 * b + n, c * P:(c + 1) * P],
                                       ps[:, 6 + q % 2, 0:n * P].rearrange("p (k n) -> p k n", k=n), ACT.Copy, scale=K_UP).then_inc(kt_hi, 1)

                for c in range(4):
                    u, q = c % 2, 4 * kh + c
                    for s in range(2):
                        conv_act(act, J_K[kh] + 1, c, s)
                    if c:
                        k_turn(c - 1)
                    act.wait_ge(km_ready, q + 1)
                    act.wait_ge(ke_zero, 4)
                    if q >= 2:
                        act.wait_ge(kt_mm, 3 * (q - 1))
                    act.activation(k_exp[u][:, 0:N], banks(3 * ((c + kh) % 2), 3)[:, 0:N], ACT.Exp, bias=kmax[:, u, 1:2],
                                   scale=1.0 / (X_UP * W_UP), accum_out=ks[:, q:q + 1]).then_inc(ke_ready, 1)

                def v_high(t, u, i, s):
                    if i is not None:
                        conv_act(act, J_V[kh] + 1, i, s)
                    if isinstance(t, int) and t == 0:
                        k_turn(3)
                    act.wait_ge(g_done, G_BASE[J_V[kh]] + t + 1)
                    act.activation(kv[1][0][:, ds(t, 1), :], ps[:, BANK[J_V[kh]] + u, :], ACT.Copy, scale=H_UP / (X_UP * W_UP)).then_inc(g_hi, 1)

                tiles(act, v_high)
                act.wait_ge(ctx_mm, 4 * (kh + 1))
                for b in range(2):
                    r = slice(64 * b, 64 * b + 64)
                    act.activation(ctxt[0][r, 4 * kh:4 * kh + 4, r], ps[r, 2 + 3 * kh, :].rearrange("p (k n) -> p k n", k=4)[:, :, r],
                                   ACT.Copy, scale=C_UP / (H_UP * K_UP)).then_inc(ctx_hi, 1)

            for u in range(2):
                act.wait_ge(x1_st[u], 16 * NT // 2)

            def q_turn(qh, t, u):
                act.wait_ge(q_mm, NT * qh + t + 1)
                act.activation(qt[0][:, 4 * qh:4 * qh + 4, ds(t * P, P)], ps[:, 6 + u, :].rearrange("p (k n) -> p k n", k=4),
                               ACT.Copy, scale=Q_UP).then_inc(q_hi, 1)

            for qh in range(2):
                def q_body(t, u, i, s):
                    if i is not None and qh == 0:
                        conv_act(act, J_Q + 1, i, s)
                    if i is not None and qh == 1:
                        for b in range(2):
                            pconv_act(act, 2 * i + s, b)
                    act.wait_ge(g_free, G_BASE[J_Q + qh] + t + 3)
                    act.activation(q_s[u][:, :], q_s[u][:, :], ACT.Exp, scale=1.0 / (X_UP * W_UP)).then_inc(q_exp, 1)
                    if not (isinstance(t, int) and t == 0):
                        q_turn(qh, t - 1, 1 - u)
                    elif qh == 1:
                        q_turn(0, NT - 1, 1)
                    if i is not None and qh == 1:
                        c = 2 * i + s
                        for b in range(2):
                            act.wait_ge(m_mm, 2 * c + b + 1)
                            act.wait_ge(rks_ready, 1)
                            act.activation(m_sb[0][:, ds(c, 1), b * HALF:(b + 1) * HALF], ps[:, b, :], ACT.Copy,
                                           scale=rks[:, ds(c, 1)]).then_inc(m_hi, 1)

                tiles(act, q_body)

            def mix_act(t, u, i, s):
                n = turns(t, u, i, s)
                if i is not None:
                    fconv_act(act, i, s)
                act.wait_ge(ln2_mv, t + 1)
                act.activation(sd[:, u, :], mv[:, u, 1:2], ACT.Sqrt, bias=eps_ln[:, 0:1]).then_inc(ln2_sd, 1)
                act.wait_ge(ln2_nb, t + 1)
                act.wait_ge(xf_mm, 2 * t + 2)
                act.wait_ge(xf_st[u], 16 * n)
                act.activation(xfm[u][:, :], x2m[u][:, :], ACT.Identity, bias=nbias[:, u, :], scale=rstd[:, u, :]).then_inc(act_m, 1)
                act.wait_ge(act_m, 2 * t + 1)
                act.activation(sqj[:, :], xfm[u][:, :], ACT.Square, accum_out=ssq[:, 0:1]).then_inc(act_m, 1)
                act.wait_ge(act_m, 2 * t + 2)
                act.activation(ssq[:, 1:2], ssq[:, 0:1], ACT.Sqrt, bias=eps_rms[:, 0:1], scale=1.0 / D).then_inc(rms_sd, 1)
                for b in range(2):
                    act.wait_ge(xf_mm, 2 * t + b + 5)
                    if not (isinstance(t, int) and t == 0):
                        act.wait_ge(lg_mm, t)
                    act.activation(xft[:, 4 * b:4 * b + 4, :], ps[:, 4 + b, :].rearrange("p (k n) -> p k n", k=4), ACT.Copy).then_inc(xft_ready, 1)

            q_turn(1, NT - 1, 1)
            tiles(act, mix_act)
            act.wait_ge(wd_ready, 1)
            act.activation(wexp[:, :], wdiff[:, :], ACT.Exp).then_inc(we_ready, 1)

            s_reg = act.alloc_register("act_slot")

            def xgt_high(s):
                for b in range(2):
                    act.wait_ge(xg_mm, 2 * s + b + 1)
                    act.activation(xgt[0][:, 4 * b:4 * b + 4, :], ps[:, b, :].rearrange("p (k n) -> p k n", k=4), ACT.Copy,
                                   scale=F_UP).then_inc(xgt_hi, 1)

            def hidt_high(s):
                act.wait_ge(hid_mm, s + 1)
                act.activation(hidt[0][:, :, :], ps[:, 6, :].rearrange("p (k n) -> p k n", k=KF), ACT.Copy).then_inc(hidt_hi, 1)

            def store_y(s):
                act.wait_ge(y_ready, s + 1)
                act.dma_start(y_dram[ds(s * P, P), :], y_sb[:, :]).then_inc(y_st, 16)

            def slot_act(s, e, slot, first, convert, very_first=False):
                if not very_first:
                    hidt_high(s - 1)
                if convert:
                    for c in range(3 if very_first else EARLY):
                        if c == 0 and not very_first:
                            act.wait_ge(g1_done, s)
                        econv_act(act, e + 1, 1 - slot, c, c % 4)
                act.wait_ge(g1_done, s + 1)
                act.wait_ge(ab_done, 2 * s + 1)
                act.activation(ga[:, :], ga[:, :], ACT.Silu).then_inc(silu_done, 1)
                xgt_high(s + 1)
                if not very_first:
                    store_y(s - 1)
                if convert:
                    for c in range(3 if very_first else EARLY, NC):
                        if c == KD and not very_first:
                            act.wait_ge(g2_done, s)
                        econv_act(act, e + 1, 1 - slot, c, c % 4)

            act.wait_ge(lg_ready, NT)
            for u in range(2):
                act.wait_ge(xf_st[u], 16 * (NT // 2 + 1))
                act.wait_ge(x2_st[u], 16 * (NT // 2 + 1))
            act.wait_ge(pos_ready, 1)
            xgt_high(0)
            for c in range(KD, NC):
                econv_act(act, 0, 0, c, c % 4)

            def expert_act(e, slot, first=False, last=False):
                n = act.value_load(toti[0:1, 1, ds(e, 1)], min_val=1, max_val=NT)
                if first:
                    slot_act(0, e, slot, True, not last, very_first=True)
                    act.reg_mov(s_reg, 1)
                else:
                    slot_act(act.snap(s_reg, min_val=1, max_val=SLOTS - 1), e, slot, True, not last)
                    act.reg_add(s_reg, s_reg, 1)
                with act.If(n > 1):
                    with act.Fori(1, n):
                        slot_act(act.snap(s_reg, min_val=1, max_val=SLOTS - 1), e, slot, False, False)
                        act.reg_add(s_reg, s_reg, 1)

            expert_act(0, 0, first=True)
            expert_act(1, 1)
            with act.Fori(1, NE // 2 - 1) as j:
                expert_act(2 * j, 0)
                expert_act(2 * j + 1, 1)
            expert_act(NE - 2, 0)
            expert_act(NE - 1, 1, last=True)
            s_end = act.snap(s_reg, min_val=1, max_val=SLOTS)
            hidt_high(s_end - 1)
            store_y(s_end - 1)

        @block.tensor
        def _(pe):
            pe.wait_ge(const_set, 19)
            pe.sem_inc(xt_done, 4)
            pe.sem_inc(g_free, 2)
            for s_ in (cnt_ready, gnn_free, x2_ready, qt_done):
                pe.sem_inc(s_, 2)
            pe.sem_inc(oh_free, 2 * UNIT)

            def ranges_in():
                pe.wait_ge(idx_ready, 1)
                for q in range(2):
                    for g in range(EG):
                        mm = pe.matmul(ps[0:16, 6 + q, g * P:(g + 1) * P], urep[:, q, g, :], ident[:, :], start=True, stop=True)
                mm.then_inc(win_mm, 1)

            def ranges_out():
                pe.wait_ge(win_ready, 1)
                for q in range(2):
                    mm = pe.matmul(ps[0:1, 6, 16 * q:16 * q + 16], win[0:16, q:q + 1], ident[0:16, 0:16], start=True, stop=True)
                mm.then_inc(win_mm, 1)

            def turn_x(t, u):
                pe.wait_ge(xn_ready, t + 1)
                pe.wait_ge(xt_done, 2 * t + 2)
                for b in range(2):
                    for k in range(4):
                        mm = pe.transpose(ps[:, 2 * u + b, k * P:(k + 1) * P], x_n[u][:, (4 * b + k) * P:(4 * b + k + 1) * P], ident[:, :])
                    mm.then_inc(xn_turned, 1)

            def gemm(j, t, u, beside=None):
                g = G_BASE[j] + t
                pe.wait_ge(g_free, g + 1)
                for k in range(KD):
                    if j == 0 and isinstance(t, int) and t == 0:
                        pe.wait_ge(w_done, k + 3)
                    mm = split_mm(pe, [ps[:, BANK[j] + u, :]], [xt[p][:, k, ds(t * P, P)] for p in range(2)],
                                  [[w_sb[j % 2][p][:, k, :] for p in range(2)]], k == 0, k == KD - 1)
                    if k == KD - 1:
                        mm.then_inc(g_done, 1)
                    if beside:
                        beside(k)

            turn_x(0, 0)
            for half in range(2):
                if half == 1:
                    pe.wait_ge(w_done, KD * (half + 1) + 2)

                def h_body(t, u, i, s):
                    if half == 0:
                        if not (isinstance(t, int) and t == NT - 1):
                            turn_x(t + 1, 1 - u)
                        pe.wait_ge(xt_done, 2 * t + 6)
                    gemm(half, t, u)
                    if half == 1 and isinstance(t, int):
                        ranges_in() if t == 0 else ranges_out()

                tiles(pe, h_body)
            pe.wait_ge(alrep_ready, 1)
            for t in range(NT):
                mm = pe.matmul(ps[:, (6, 7, 4)[t // 4], t % 4 * P:(t % 4 + 1) * P], al_rep[:, t, :], ident[:, :], start=True, stop=True, skip_group_check=True)
            mm.then_inc(alrow_mm, 1)
            r = pe.alloc_register("pe_units")
            pe.reg_mov(r, 0)
            pe.wait_ge(win_ready, 2)
            pe.wait_ge(g_free, 22)
            chunks = ((0, 0, HALF), (1, HALF, HALF), (2, 2 * HALF, NP - 2 * HALF))

            def window_pe(w, wu, i, s_):
                if isinstance(w, int) and w == 0:
                    pe.wait_ge(cnt_ready, 1)
                else:
                    pe.wait_ge(alrow_ready, 1)
                    pe.wait_ge(cnt_ready, w + 1)
                steps = pe.value_load(lohi[0:1, ds(16 + w, 1)], min_val=MIN_STEPS, max_val=ER)
                for b, c0, n in chunks:
                    pe.matmul(ps[:, 3 * wu + b, 0:n], zero_h[:, 0:P], zero_h[:, 0:n], start=True, stop=False, skip_group_check=True)
                with pe.Fori(0, steps):
                    n_u = pe.snap(r, min_val=0, max_val=NT * ER)
                    for u in range(UNIT):
                        pe.wait_ge(oh_ready, UNIT * n_u + u + 1)
                        if u == DVE_TILES:
                            pe.wait_ge(oh_act_ready, n_u + 1)
                        lhs = oh_dst[u][:, :] if u < DVE_TILES else oh_dst_act[:, ds((n_u % 2) * (UNIT - DVE_TILES) + u - DVE_TILES, 1), :]
                        for b, c0, n in chunks:
                            n = min(n, N - c0)
                            mm = pe.matmul(ps[:, 3 * wu + b, 0:n], lhs, oh_src[u][:, c0:c0 + n],
                                           start=False, stop=False, skip_group_check=True)
                        mm.then_inc(oh_free, 1)
                    pe.reg_add(r, r, 1)
                pe.matmul(ps[:, 3 * wu + 2, 0:2], zero_h[:, 0:P], zero_h[:, 0:2], start=False, stop=True,
                          skip_group_check=True).then_inc(win_done, 1)

            tiles(pe, window_pe)
            pe.wait_ge(adj_done, NT + 1)

            def gnn(t, u):
                pe.wait_ge(gnn_free, t + 1)
                for k in range(NT):
                    if isinstance(t, int) and t == 0 and k == NT - 1:
                        pe.wait_ge(adj_done, NT + 2)
                    lhs = [adj[p][:, k, ds(t * P, P)] for p in range(2)]
                    split_mm(pe, [ps[:, 3 * u + b, :] for b in range(2)], lhs,
                             [[h[p][:, k, b * HALF:(b + 1) * HALF] for p in range(2)] for b in range(2)], k == 0, k == NT - 1)
                    for p in range(2):
                        mm = pe.matmul(ps[:, 3 * u + 2, 0:2], lhs[p], ones_h[:, :], start=(k == 0 and p == 0), stop=(k == NT - 1 and p == 1),
                                       skip_group_check=True)
                mm.then_inc(gnn_done, 1)

            tiles(pe, lambda t, u, i, s: gnn(t, u))

            K_TURN, V_TURN = (3, 4, 5), (5, 6, 7)
            for kh in range(2):
                j = J_K[kh]

                def k_turn(c, b):
                    n, q = (4, 4, 2)[b], 12 * kh + 3 * c + b
                    pe.wait_ge(ke_ready, 4 * kh + c + 1)
                    if q >= 2:
                        pe.wait_ge(kt_done, q - 1)
                    for k in range(n):
                        mm = pe.transpose(ps[:, 6 + q % 2, k * P:(k + 1) * P], k_exp[c % 2][:, (4 * b + k) * P:(4 * b + k + 1) * P], ident[:, :])
                    mm.then_inc(kt_mm, 1)

                pe.wait_ge(w_done, KD * (j + 1) + 2)
                for c in range(4):
                    bank = 3 * ((c + kh) % 2)
                    if kh == 0 and c < 2:
                        pe.wait_ge(gnn_free, NT + 1 + c)
                    if kh == 1 and c == 0:
                        pe.wait_ge(ke_ready, 4)
                    if kh == 1 and c == 1:
                        pe.wait_ge(ctx_done, 2)
                        pe.wait_ge(g_free, G_BASE[J_V[0]] + NT + 2)
                    if c >= 2:
                        pe.wait_ge(ke_ready, 4 * kh + c - 1)
                    for k in range(KD):
                        lhs = [w_sb[j % 2][p][:, k, c * P:(c + 1) * P] for p in range(2)]
                        mm = split_mm(pe, [ps[:, bank + b, 0:min(n, N - c0)] for b, c0, n in chunks], lhs,
                                      [[xt[p][:, k, c0:min(c0 + n, N)] for p in range(2)] for b, c0, n in chunks], k == 0, k == KD - 1)
                        if k == KD - 1:
                            mm.then_inc(k_done, 1)
                        if c and k in K_TURN:
                            k_turn(c - 1, K_TURN.index(k))

                def v_body(t, u, i, s):
                    gemm(J_V[kh], t, u, (lambda k: k in V_TURN and k_turn(3, V_TURN.index(k))) if isinstance(t, int) and t == 0 else None)

                pe.wait_ge(w_done, KD * (J_V[kh] + 1) + 2)
                pe.wait_ge(ke_ready, 4 * kh + 3)
                tiles(pe, v_body)
                pe.wait_ge(kt_done, 12 * kh + 12)
                pe.wait_ge(g_free, G_BASE[J_V[kh]] + NT + 1)
                with pe.Fori(0, 4) as c:
                    for t in range(NT):
                        if t == NT - 1:
                            pe.wait_ge(g_free, G_BASE[J_V[kh]] + NT + 2)
                        mm = split_mm(pe, [ps[:, 2 + 3 * kh, ds(c * P, P)]], [kv[1][p][:, t, ds(c * P, P)] for p in range(2)],
                                      [[kv[0][p][:, t, ds(c * P, P)] for p in range(2)]], t == 0, t == NT - 1)
                    mm.then_inc(ctx_mm, 1)

            def project(c):
                for b in range(2):
                    pe.wait_ge(w_done, KD * J_P + 2 * c + b + 3)
                    pe.wait_ge(m_done, 2 * c + b + 1)
                    split_mm(pe, [ps[:, b, :]], [ctxt[p][:, ds(c, 1), :] for p in range(2)],
                             [[w_proj[b][p][:, ds(c, 1), :] for p in range(2)]], True, True).then_inc(m_mm, 1)

            def q_turn(g, u):
                pe.wait_ge(q_norm, g + 1)
                pe.wait_ge(qt_done, g + 1)
                for k in range(4):
                    mm = pe.transpose(ps[:, 6 + u, k * P:(k + 1) * P], q_s[u][:, k * P:(k + 1) * P], ident[:, :])
                mm.then_inc(q_mm, 1)

            for qh in range(2):
                if qh == 1:
                    pe.wait_ge(ctx_done, 4)
                pe.wait_ge(w_done, KD * (J_Q + qh + 1) + 2)

                def q_body(t, u, i, s):
                    gemm(J_Q + qh, t, u)
                    if not (isinstance(t, int) and t == 0):
                        q_turn(NT * qh + t - 1, 1 - u)
                    elif qh == 1:
                        q_turn(NT - 1, 1)
                    if i is not None and qh == 1:
                        project(2 * i + s)

                tiles(pe, q_body)
            pe.wait_ge(m_done, 2 * KD + 2)

            def mix(t, u, part):
                if part.start == 0:
                    pe.wait_ge(x2_ready, t + 1)
                for c in range(KD)[part]:
                    mm = split_mm(pe, [ps[:, 2 * u + b, :] for b in range(2)], [qt[p][:, c, ds(t * P, P)] for p in range(2)],
                                  [[m_sb[p][:, c, b * HALF:(b + 1) * HALF] for p in range(2)] for b in range(2)], c == 0, c == KD - 1)
                if part.stop == KD:
                    mm.then_inc(mix_done, 1)

            def route_turn(t, u):
                pe.wait_ge(xf_ready, t + 1)
                for b in range(2):
                    if not (isinstance(t, int) and t == 0):
                        pe.wait_ge(xft_ready, 2 * t)
                    for k in range(4):
                        mm = pe.transpose(ps[:, 4 + b, k * P:(k + 1) * P], xfm[u][:, (4 * b + k) * P:(4 * b + k + 1) * P], ident[:, :])
                    mm.then_inc(xf_mm, 1)

            def route(t):
                pe.wait_ge(xft_ready, 2 * t + 2)
                if not (isinstance(t, int) and t == 0):
                    pe.wait_ge(lg_ready, t)
                for k in range(KD):
                    mm = pe.matmul(ps[:, 6, 0:NE], xft[:, k, :], wg_sb[:, k, :], start=(k == 0), stop=(k == KD - 1))
                mm.then_inc(lg_mm, 1)

            def mix_body(t, u, i, s):
                if isinstance(t, int) and t == NT - 1:
                    pe.wait_ge(qt_done, 2 * NT + 2)
                mix(t, u, slice(0, KD - 1))
                if isinstance(t, int) and t == 0:
                    q_turn(2 * NT - 1, 1)
                    pe.wait_ge(g_free, G_BASE[J_Q + 1] + NT + 2)
                if not (isinstance(t, int) and t == 0):
                    route_turn(t - 1, 1 - u)
                mix(t, u, slice(KD - 1, KD))
                if not (isinstance(t, int) and t == 0):
                    route(t - 1)

            tiles(pe, mix_body)
            route_turn(NT - 1, 1)
            route(NT - 1)
            pe.wait_ge(mask_ready, 1)
            pe.matmul(ps[:, 7, 0:NT * NE], tri[:, :], mask[:, :, :].rearrange("p t e -> p (t e)"), start=True, stop=False, skip_group_check=True)
            pe.matmul(ps[:, 7, 0:NT * NE], ones_b[:, :], before[:, 0:NT, :].rearrange("p t e -> p (t e)"), start=False, stop=True, skip_group_check=True)
            pe.matmul(ps[:, 7, 128:128 + NE], ones_b[:, :], before[:, NT, :], start=True, stop=True, skip_group_check=True).then_inc(rank_mm, 1)

            for q in range(TOPK * NT):
                pe.wait_ge(place_ready, q + 1)
                mm = pe.matmul(ps[:, 7, 256:256 + SLOTS + 1], oh_row[:, q, :], oh_tile[:, q, :], start=(q == 0), stop=(q == TOPK * NT - 1),
                               skip_group_check=True)
            mm.then_inc(place_mm, 1)

            s_reg = pe.alloc_register("pe_slot")

            def turn_g(s):
                if isinstance(s, int) and s == 1:
                    pe.wait_ge(xg_second_ld, 16)
                else:
                    pe.wait_ge(xg_ld, 16 * (1 if isinstance(s, int) else s))
                if not (isinstance(s, int) and s == 0):
                    pe.wait_ge(xgt_done, 2 * s)
                for b in range(2):
                    for k in range(4):
                        mm = pe.transpose(ps[:, b, k * P:(k + 1) * P], (xg_second if isinstance(s, int) and s == 1 else xg)[:, (4 * b + k) * P:(4 * b + k + 1) * P], ident[:, :])
                    mm.then_inc(xg_mm, 1)

            def turn_hid(s):
                pe.wait_ge(hid_ready, s + 1)
                if not (isinstance(s, int) and s == 0):
                    pe.wait_ge(hidt_done, s)
                for k in range(KF):
                    mm = pe.transpose(ps[:, 6, k * P:(k + 1) * P], hid[:, k * P:(k + 1) * P], ident[:, :])
                mm.then_inc(hid_mm, 1)

            def up(s, slot):
                pe.wait_ge(xgt_done, 2 * s + 2)
                if not (isinstance(s, int) and s == 0):
                    pe.wait_ge(ab_done, 2 * s)
                for k in range(KD):
                    mm = split_mm(pe, [ps[:, 2 + b, :] for b in range(2)], [xgt[p][:, k, :] for p in range(2)],
                                  [[ew[slot][p][:, k, b * HALF:(b + 1) * HALF] for p in range(2)] for b in range(2)], k == 0, k == KD - 1)
                mm.then_inc(g1_done, 1)

            def down(s, slot, e):
                pe.wait_ge(ew_done, NC * e + NC + 4)
                pe.wait_ge(hidt_done, s + 1)
                if not (isinstance(s, int) and s == 0):
                    pe.wait_ge(y_ready, s)
                for k in range(KF):
                    mm = split_mm(pe, [ps[:, 4 + b, :] for b in range(2)], [hidt[p][:, k, :] for p in range(2)],
                                  [[ew[slot][p][:, KD + k, b * HALF:(b + 1) * HALF] for p in range(2)] for b in range(2)], k == 0, k == KF - 1)
                mm.then_inc(g2_done, 1)

            turn_g(0)

            def expert_pe(e, slot, first=False):
                n = pe.value_load(toti[0:1, 1, ds(e, 1)], min_val=1, max_val=NT)
                pe.wait_ge(ew_done, NC * e + KD + 4)
                if first:
                    up(0, slot)
                    turn_g(1)
                    pe.reg_mov(s_reg, 1)
                else:
                    s = pe.snap(s_reg, min_val=1, max_val=SLOTS - 1)
                    turn_g(s + 1)
                    turn_hid(s - 1)
                    up(s, slot)
                    down(s - 1, 1 - slot, e - 1)
                    pe.reg_add(s_reg, s_reg, 1)
                with pe.If(n > 1):
                    with pe.Fori(1, n):
                        s = pe.snap(s_reg, min_val=1, max_val=SLOTS - 1)
                        turn_g(s + 1)
                        turn_hid(s - 1)
                        up(s, slot)
                        down(s - 1, slot, e)
                        pe.reg_add(s_reg, s_reg, 1)

            expert_pe(0, 0, first=True)
            expert_pe(1, 1)
            with pe.Fori(1, NE // 2) as j:
                expert_pe(2 * j, 0)
                expert_pe(2 * j + 1, 1)
            s_end = pe.snap(s_reg, min_val=1, max_val=SLOTS)
            turn_hid(s_end - 1)
            down(s_end - 1, 1, NE - 1)

        @block.vector
        def _(dve):
            dve.sem_inc(adj_done, 2)
            dve.sem_inc(m_done, 2)
            dve.sem_inc(w_done, 2)

            def chain(s, per):
                state = {"n": 0}

                def start(r):
                    state["r"], state["n"] = r, 0

                def link(ins):
                    state["n"] += 1
                    assert state["n"] <= per
                    ins.then_inc(s, 1)
                    dve.wait_ge(s, state["r"] * per + state["n"])
                return start, link

            def ln_stats(t, u, n):
                dve.wait_ge(xin_ld[u], 16 * n)
                r = 2 * t
                for b in range(2):
                    ins = dve.bn_stats(stats[:, u, 6 * b:6 * b + 6], x_in[u][:, b * HALF:(b + 1) * HALF])
                ins.then_inc(dve_ln, 1)
                wait_alone(dve, dve_ln, r + 1)
                dve.bn_aggr(mv[:, u, :], stats[:, u, :]).then_inc(ln_mv, 1)

            def ln_scale(t, u):
                r = 2 * t
                dve.wait_ge(ln_mv, t + 1)
                dve.wait_ge(ln_sd, t + 1)
                dve.reciprocal(rstd[:, u, :], sd[:, u, :]).then_inc(dve_ln, 1)
                dve.wait_ge(dve_ln, r + 2)
                dve.scalar_tensor_tensor(nbias[:, u, :], mv[:, u, 0:1], -1.0, rstd[:, u, :], ALU.mult, ALU.mult).then_inc(ln_nb, 1)

            def xt_low(t, u):
                for b in range(2):
                    dve.wait_ge(xt_hi, 2 * t + b + 1)
                    o = slice(4 * b, 4 * b + 4)
                    dve.scalar_tensor_tensor(xt[1][:, o, ds(t * P, P)], ps[:, 2 * u + b, :].rearrange("p (k n) -> p k n", k=4), X_UP,
                                             xt[0][:, o, ds(t * P, P)], ALU.mult, ALU.subtract).then_inc(xt_done, 1)

            start, link = chain(dve_c, 100)

            def indices():
                start(0)
                dve.wait_ge(const_ld, 16 * 7)
                dve.wait_ge(const_set, 19)
                dve.tensor_copy(src_f[:, :], idx_in[:, 0, :])
                dve.tensor_copy(dst_f[:, :], idx_in[:, 1, :])
                dve.tensor_scalar(dst_neg[:, :], idx_in[:, 1, :], -1.0, None, ALU.mult)
                link(dve.tensor_copy(rows_f[:, :, :], rows_i[:, :, :]))
                dve.tensor_reduce(ured[:, 0, :], rows_f[:, :, :], AX, ALU.min)
                link(dve.tensor_reduce(ured[:, 1, :], rows_f[:, :, :], AX, ALU.max))
                for q in range(2):
                    for g in range(EG):
                        ins = dve.tensor_scalar(urep[:, q, g, :], ones_f[:, 0:16], ured[:, q, g:g + 1], None, ALU.mult)
                ins.then_inc(idx_ready, 1)

            def ranges():
                dve.wait_ge(win_mm, 1)
                mn, mx = ps[0:16, 6, 0:ER], ps[0:16, 7, 0:ER]
                link(dve.tensor_scalar(win[:, 2:3], iota_w[:, 0:1], float(P), None, ALU.add))
                link(dve.tensor_scalar(rtile[:, 1, :], mn, win[:, 2:3], None, ALU.is_lt))
                link(dve.scalar_tensor_tensor(rtile[:, 2, :], mx, iota_w[:, 0:1], rtile[:, 1, :], ALU.is_ge, ALU.mult))
                link(dve.scalar_tensor_tensor(rtile[:, 1, :], iota_u[:, :], -BIG, rtile[:, 2, :], ALU.add, ALU.mult))
                link(dve.scalar_tensor_tensor(rtile[:, 3, :], iota_u[:, :], 1.0, rtile[:, 2, :], ALU.add, ALU.mult))
                link(dve.tensor_reduce(win[:, 3:4], rtile[:, 1, :], AX, ALU.min))
                link(dve.tensor_reduce(win[:, 4:5], rtile[:, 3, :], AX, ALU.max))
                link(dve.tensor_scalar(win[:, 5:6], win[:, 3:4], BIG, None, ALU.add))
                link(dve.tensor_scalar(win[:, 0:1], win[:, 5:6], float(ET - MIN_STEPS * UNIT), None, ALU.min))
                link(dve.tensor_tensor(win[:, 6:7], win[:, 4:5], win[:, 0:1], ALU.subtract))
                link(dve.tensor_scalar(rtile[:, 2, :], iota_u[:, :], float(UNIT), win[:, 6:7], ALU.mult, ALU.is_lt))
                link(dve.tensor_reduce(win[:, 7:8], rtile[:, 2, :], AX, ALU.add))
                dve.tensor_scalar(win[:, 1:2], win[:, 7:8], float(MIN_STEPS), None, ALU.max).then_inc(win_ready, 1)

            def h_low(half):
                def body(t, u, i, s):
                    if half == 0 and not (isinstance(t, int) and t > NT - 3):
                        ln_stats(t + 2, u, turns(t, u, i, s) + 1)
                        ln_scale(t + 2, u)
                    if half == 0 and not (isinstance(t, int) and t == NT - 1):
                        xt_low(t + 1, 1 - u)
                    if i is not None:
                        conv_dve(dve, half + 1, i, s)
                    c = slice(half * HALF, (half + 1) * HALF)
                    dve.wait_ge(g_hi, G_BASE[half] + t + 1)
                    dve.scalar_tensor_tensor(h[1][:, ds(t, 1), c], ps[:, 4 + u, :], H_UP / (X_UP * W_UP), h[0][:, ds(t, 1), c],
                                             ALU.mult, ALU.subtract)
                    dve.wait_ge(g_free, G_BASE[half] + t + 2)
                    for q in range(2):
                        ins = dve.scalar_tensor_tensor(junk[q][:, :], ps[:, 4 + u, :], 1.0 / (X_UP * W_UP), a_b[:, q, c], ALU.mult, ALU.mult,
                                                       accum_out=al_part[:, q, half, ds(t, 1)])
                    ins.then_inc(g_free, 1)
                    if half == 1 and isinstance(t, int) and t == 0:
                        ranges()
                return body

            ln_stats(0, 0, 1)
            ln_scale(0, 0)
            for g in range(KD // 2):
                dve.wait_ge(w_hi, 2 * g + 2)
                dve.scalar_tensor_tensor(w_sb[0][1][:, 2 * g:2 * g + 2, :], stage_h[:, 2 * g:2 * g + 2, :], W_UP,
                                         w_sb[0][0][:, 2 * g:2 * g + 2, :], ALU.mult, ALU.subtract).then_inc(w_done, 2)
                if g == 0:
                    ln_stats(1, 1, 1)
                    ln_scale(1, 1)
                    xt_low(0, 0)
            dve.wait_ge(a_ld, 32)
            tiles(dve, h_low(0), 3)
            indices()
            tiles(dve, h_low(1))
            dve.wait_ge(g_free, 22)
            dve.wait_ge(win_mm, 2)
            dve.tensor_copy(lohi[0:1, :], ps[0:1, 6, 0:32]).then_inc(win_ready, 1)
            link(dve.tensor_tensor(al_ar[:, :, :], al_part[:, :, 0, :], al_part[:, :, 1, :], ALU.add))
            for q, factor in enumerate((SLOPE, 1.0 - SLOPE)):
                dve.tensor_scalar(ar_slope[:, q, :], al_ar[:, 1, :], factor, None, ALU.mult)
            dve.tensor_copy(al_rep[:, :, :], al_ar[:, 0, :].to_broadcast([P, NT, P])).then_inc(alrep_ready, 1)

            r, tile_r = dve.alloc_register("dve_steps"), dve.alloc_register("dve_tile")
            dve.reg_mov(r, 0)
            dve.wait_ge(win_ready, 2)

            def one_hots(w):
                first = dve.snap(tile_r, min_val=0, max_val=ET - UNIT)
                n_u = dve.snap(r, min_val=0, max_val=NT * ER)
                for u in range(UNIT):
                    dve.wait_ge(oh_free, UNIT * n_u + u + 1 + UNIT)
                    ins = dve.tensor_scalar(oh_src[u][:, 0:N], iota_n[:, 0:N], src_f[:, ds(first + u, 1)], None, ALU.is_equal)
                    if u < DVE_TILES:
                        ins = dve.tensor_scalar(oh_dst[u][:, :], iota_n[:, ds(w * P, P)], dst_f[:, ds(first + u, 1)], None, ALU.is_equal)
                    ins.then_inc(oh_ready, 1)
                dve.reg_add(r, r, 1)
                dve.reg_add(tile_r, tile_r, UNIT)

            def weigh(w, wu):
                dve.wait_ge(e_ready, w + 1)
                dve.wait_ge(win_done, w + 1)
                dve.tensor_tensor(edge[wu][:, :], edge[wu][:, :], banks(3 * wu, 3)[:, 0:NP], ALU.mult).then_inc(cnt_ready, 1)

            def adj_low(w, wu):
                dve.wait_ge(adj_hi, w + 1)
                dve.wait_ge(cnt_ready, w + 3)
                dve.tensor_tensor(adj[1][:, ds(w, 1), :], edge[wu][:, :], adj[0][:, ds(w, 1), :], ALU.subtract).then_inc(adj_done, 1)

            def window_dve(w, wu, i, s_):
                lo = dve.value_load(lohi[0:1, ds(w, 1)], min_val=0, max_val=ER - 1)
                steps = dve.value_load(lohi[0:1, ds(16 + w, 1)], min_val=MIN_STEPS, max_val=ER)
                dve.reg_mov(tile_r, lo)
                one_hots(w)
                if not (isinstance(w, int) and w == 0):
                    weigh(w - 1, 1 - wu)
                with dve.Fori(1, steps):
                    one_hots(w)
                if not (isinstance(w, int) and w == 0):
                    adj_low(w - 1, 1 - wu)

            tiles(dve, window_dve)
            weigh(NT - 1, 1)
            adj_low(NT - 1, 1)

            def gnn(t, u, i, s):
                start, link = chain(dve_g, 5)
                start(t)
                dve.wait_ge(gnn_done, t + 1)
                link(dve.tensor_scalar(rsum[:, u, 0:1], ps[:, 3 * u + 2, 0:1], EPS_GNN, None, ALU.add))
                link(dve.reciprocal(rsum[:, u, 1:2], rsum[:, u, 0:1]))
                link(dve.tensor_scalar(rsum[:, u, 2:3], rsum[:, u, 1:2], 1.0 / H_UP, None, ALU.mult))
                dve.tensor_scalar(neg[:, :], banks(3 * u, 2), rsum[:, u, 2:3], 0.0, ALU.mult, ALU.min).then_inc(neg_ready, 1)
                dve.tensor_scalar(poz[:, :], banks(3 * u, 2), rsum[:, u, 2:3], 0.0, ALU.mult, ALU.max).then_inc(gnn_free, 1)
                dve.wait_ge(x1_ld[u], 16 * turns(t, u, i, s))
                link(dve.tensor_tensor(x1[u][:, :], x1[u][:, :], bproj_b[:, :], ALU.add))
                dve.wait_ge(gnn_free, t + 3)
                link(dve.tensor_tensor(x1[u][:, :], x1[u][:, :], poz[:, :], ALU.add))
                dve.wait_ge(neg_exp, t + 1)
                dve.scalar_tensor_tensor(x1[u][:, :], neg[:, :], -1.0, x1[u][:, :], ALU.add, ALU.add).then_inc(x1_ready, 1)

            tiles(dve, gnn)

            for kh in range(2):
                def k_turn(c):
                    for b, n in enumerate((4, 4, 2)):
                        q = 12 * kh + 3 * c + b
                        o = (slice(None), slice(4 * b, 4 * b + n), slice(c * P, (c + 1) * P))
                        dve.wait_ge(kt_hi, 3 * (4 * kh + c) + b + 1)
                        dve.scalar_tensor_tensor(kv[0][1][o], ps[:, 6 + q % 2, 0:n * P].rearrange("p (k n) -> p k n", k=n), K_UP,
                                                 kv[0][0][o], ALU.mult, ALU.subtract).then_inc(kt_done, 1)

                for c in range(4):
                    u, q = c % 2, 4 * kh + c
                    for s in range(2):
                        conv_dve(dve, J_K[kh] + 1, c, s)
                    if c:
                        k_turn(c - 1)
                    dve.wait_ge(k_done, q + 1)
                    dve.tensor_reduce(kmax[:, u, 0:1], banks(3 * ((c + kh) % 2), 3)[:, 0:N], AX, ALU.max).then_inc(dve_k, 1)
                    dve.wait_ge(dve_k, q + 1)
                    dve.tensor_scalar(kmax[:, u, 1:2], kmax[:, u, 0:1], -1.0 / (X_UP * W_UP), None, ALU.mult).then_inc(km_ready, 1)

                def v_low(t, u, i, s):
                    if i is not None:
                        conv_dve(dve, J_V[kh] + 1, i, s)
                    if isinstance(t, int) and t == 0:
                        k_turn(3)
                    dve.wait_ge(g_hi, 20 + NT * kh + t + 1)
                    dve.scalar_tensor_tensor(kv[1][1][:, ds(t, 1), :], ps[:, BANK[J_V[kh]] + u, :], H_UP / (X_UP * W_UP), kv[1][0][:, ds(t, 1), :],
                                             ALU.mult, ALU.subtract).then_inc(g_free, 1)

                tiles(dve, v_low)
                for b in range(2):
                    r_ = slice(64 * b, 64 * b + 64)
                    dve.wait_ge(ctx_hi, 2 * kh + 2)
                    dve.scalar_tensor_tensor(ctxt[1][r_, 4 * kh:4 * kh + 4, r_], ps[r_, 2 + 3 * kh, :].rearrange("p (k n) -> p k n", k=4)[:, :, r_],
                                             C_UP / (H_UP * K_UP), ctxt[0][r_, 4 * kh:4 * kh + 4, r_], ALU.mult, ALU.subtract).then_inc(ctx_done, 1)
            dve.wait_ge(ke_ready, 8)
            dve.reciprocal(rks[:, :], ks[:, :]).then_inc(rks_ready, 1)

            for u in range(2):
                dve.wait_ge(x1_st[u], 16 * NT // 2)

            def q_turn(qh, t, u):
                o = (slice(None), slice(4 * qh, 4 * qh + 4), ds(t * P, P))
                dve.wait_ge(q_hi, NT * qh + t + 1)
                dve.scalar_tensor_tensor(qt[1][o], ps[:, 6 + u, :].rearrange("p (k n) -> p k n", k=4), Q_UP, qt[0][o],
                                         ALU.mult, ALU.subtract).then_inc(qt_done, 1)

            for qh in range(2):
                def q_body(t, u, i, s):
                    start, link = chain(dve_q, 3)
                    start(NT * qh + t)
                    if i is not None and qh == 0:
                        conv_dve(dve, J_Q + 1, i, s)
                    if i is not None and qh == 1:
                        for b in range(2):
                            pconv_dve(dve, 2 * i + s, b)
                    q3 = ps[:, BANK[J_Q] + u, :].rearrange("p (h d) -> p h d", d=64)
                    s3 = q_s[u][:, :].rearrange("p (h d) -> p h d", d=64)
                    dve.wait_ge(g_done, G_BASE[J_Q + qh] + t + 1)
                    link(dve.tensor_reduce(qred[:, u, 0, :], q3, AX, ALU.max))
                    dve.tensor_tensor(s3, q3, qred[:, u, 0, :].to_broadcast([P, 8, 64]), ALU.subtract).then_inc(g_free, 1)
                    dve.wait_ge(q_exp, NT * qh + t + 1)
                    link(dve.tensor_reduce(qred[:, u, 1, :], s3, AX, ALU.add))
                    link(dve.reciprocal(qred[:, u, 2, :], qred[:, u, 1, :]))
                    dve.tensor_tensor(s3, s3, qred[:, u, 2, :].to_broadcast([P, 8, 64]), ALU.mult).then_inc(q_norm, 1)
                    if not (isinstance(t, int) and t == 0):
                        q_turn(qh, t - 1, 1 - u)
                    elif qh == 1:
                        q_turn(0, NT - 1, 1)
                    if i is not None and qh == 1:
                        c = 2 * i + s
                        for b in range(2):
                            o = (slice(None), ds(c, 1), slice(b * HALF, (b + 1) * HALF))
                            dve.wait_ge(m_hi, 2 * c + b + 1)
                            dve.scalar_tensor_tensor(m_sb[1][o], ps[:, b, :], rks[:, ds(c, 1)], m_sb[0][o], ALU.mult, ALU.subtract).then_inc(m_done, 1)

                tiles(dve, q_body)

            def top2(t):
                start, link = chain(dve_m, 6)
                start(t)
                dve.wait_ge(lg_mm, t + 1)
                dve.tensor_tensor(lg[:, :], ps[:, 6, 0:NE], bg_b[:, :], ALU.add).then_inc(lg_ready, 1)
                wait_alone(dve, lg_ready, t + 1)
                link(dve.max(top8[:, :], lg[:, :]))
                dve.tensor_tensor(wdiff[:, ds(t, 1)], top8[:, 1:2], top8[:, 0:1], ALU.subtract)
                link(dve.max_index(idx8[:, :], top8[:, :], lg[:, :]))
                link(dve.tensor_copy(idxf[:, :], idx8[:, :]))
                for k in range(TOPK):
                    last = isinstance(t, int) and t == NT - 1
                    ins = dve.tensor_scalar(onehot[:, k, t, :] if isinstance(t, int) else onehot[:, k, ds(t, 1), :], iota_e[:, :], idxf[:, k:k + 1],
                                            valid[:, 0:1] if last else None, ALU.is_equal, ALU.mult if last else ALU.bypass)
                link(ins)
                link(dve.tensor_tensor(mask[:, ds(t, 1), :], onehot[:, 0, ds(t, 1), :], onehot[:, 1, ds(t, 1), :], ALU.add))
                link(dve.tensor_tensor(before[:, ds(t + 1, 1), :], before[:, ds(t, 1), :], mask[:, ds(t, 1), :], ALU.add))

            def mix(t, u, i, s):
                n = turns(t, u, i, s)
                dve.wait_ge(mix_done, t + 1)
                dve.wait_ge(x1m_ld[u], 16 * n)
                dve.wait_ge(x2_st[u], 16 * n)
                dve.scalar_tensor_tensor(x2m[u][:, :], banks(2 * u, 2), 1.0 / (Q_UP * M_UP), x1m[u][:, :], ALU.mult, ALU.add).then_inc(x2_ready, 1)
                dve.wait_ge(x2_ready, t + 3)
                for b in range(2):
                    ins = dve.bn_stats(stats[:, u, 6 * b:6 * b + 6], x2m[u][:, b * HALF:(b + 1) * HALF])
                ins.then_inc(dve_x, 1)
                wait_alone(dve, dve_x, 3 * t + 1)
                dve.bn_aggr(mv[:, u, :], stats[:, u, :]).then_inc(ln2_mv, 1)
                dve.wait_ge(ln2_mv, t + 1)
                dve.wait_ge(ln2_sd, t + 1)
                dve.reciprocal(rstd[:, u, :], sd[:, u, :]).then_inc(dve_x, 1)
                dve.wait_ge(dve_x, 3 * t + 2)
                dve.scalar_tensor_tensor(nbias[:, u, :], mv[:, u, 0:1], -1.0, rstd[:, u, :], ALU.mult, ALU.mult).then_inc(ln2_nb, 1)
                if i is not None:
                    fconv_dve(dve, i, s)
                dve.wait_ge(rms_sd, t + 1)
                dve.reciprocal(ssq[:, 2:3], ssq[:, 1:2]).then_inc(dve_x, 1)
                dve.wait_ge(dve_x, 3 * t + 3)
                dve.scalar_tensor_tensor(xfm[u][:, :], xfm[u][:, :], ssq[:, 2:3], lnw_b[:, :], ALU.mult, ALU.mult).then_inc(xf_ready, 1)
                if not (isinstance(t, int) and t == 0):
                    top2(t - 1)

            q_turn(1, NT - 1, 1)
            tiles(dve, mix)
            top2(NT - 1)
            dve.sem_inc(mask_ready, 1)

            start, link = chain(dve_r, 24)
            start(0)
            dve.sem_inc(wd_ready, 1)
            dve.wait_ge(rank_mm, 1)
            dve.tensor_copy(rank[:, :, :], ps[:, 7, 0:NT * NE].rearrange("p (t e) -> p t e", e=NE))
            link(dve.tensor_scalar(tot[:, 0, :], ps[:, 7, 128:128 + NE], float(P - 1), None, ALU.add))
            link(dve.tensor_copy(toti[:, 0, :], tot[:, 0, :]))
            link(dve.tensor_scalar(toti[:, 2, :], toti[:, 0, :], 7, None, ALU.arith_shift_right))
            link(dve.tensor_copy(tot[:, 1, :], toti[:, 2, :]))
            link(dve.tensor_scalar(tot[:, 2, :], tot[:, 1, :], 1.0, None, ALU.max))
            link(dve.tensor_tensor_scan(tot[:, 3, :], ones_f[:, 0:NE], tot[:, 2, :], 0.0, ALU.mult, ALU.add))
            link(dve.tensor_tensor(tot[:, 4, :], tot[:, 3, :], tot[:, 2, :], ALU.subtract))
            link(dve.tensor_scalar(tot[:, 5, :], tot[:, 4, :], float(P), None, ALU.mult))
            dve.tensor_copy(toti[:, 1, :], tot[:, 2, :])
            dve.tensor_copy(toti[:, 2, :], tot[:, 3, :])
            link(dve.tensor_tensor(rank[:, :, :], rank[:, :, :], tot[:, 5:6, :].to_broadcast([P, NT, NE]), ALU.add))
            for k in range(TOPK):
                link(dve.tensor_tensor(ranked[:, :, :], rank[:, :, :], onehot[:, k, :, :], ALU.mult))
                link(dve.tensor_reduce(posf[:, k, :], ranked[:, :, :], AX, ALU.add))
            link(dve.tensor_copy(pos[:, :, :], posf[:, :, :]))
            link(dve.tensor_scalar(tile_i[:, :, :], pos[:, :, :], 7, None, ALU.arith_shift_right))
            link(dve.tensor_copy(tile_f[:, :, :], tile_i[:, :, :]))
            dve.tensor_scalar(tok[:, NT - 1:NT], tok[:, NT - 1:NT], valid[:, 0:1], None, ALU.mult)
            link(dve.scalar_tensor_tensor(row_f[:, :, :], tile_f[:, :, :], -float(P), posf[:, :, :], ALU.mult, ALU.add))
            tiles_k = oh_tile[:, :, :].rearrange("p (k t) s -> p k t s", k=TOPK)
            for k in range(TOPK):
                ins = dve.tensor_tensor(tiles_k[:, k, :, :], iota_s[:, :].unsqueeze(1).to_broadcast([P, NT, SLOTS + 1]),
                                        tile_f[:, k, :].to_broadcast([P, NT, SLOTS + 1]), ALU.is_equal)
            link(ins)
            for k in range(TOPK):
                ins = dve.tensor_tensor(tiles_k[:, k, :, :], tiles_k[:, k, :, :], tok[:, :].to_broadcast([P, NT, SLOTS + 1]), ALU.mult)
            for k in range(TOPK):
                for t in range(NT):
                    dve.tensor_scalar(oh_row[:, NT * k + t, :], iota_n[:, 0:P], row_f[:, k, t:t + 1], None, ALU.is_equal).then_inc(place_ready, 1)
            dve.sem_inc(pos_ready, 1)
            dve.wait_ge(place_mm, 1)
            dve.tensor_copy(slot_sb[:, :], ps[:, 7, 256:256 + SLOTS + 1]).then_inc(slots_ready, 1)
            dve.wait_ge(we_ready, 1)
            link(dve.tensor_scalar(wdiff[:, :], wexp[:, :], 1.0, None, ALU.add))
            link(dve.reciprocal(wts[:, 0, :], wdiff[:, :]))
            link(dve.tensor_tensor(wts[:, 1, :], wts[:, 0, :], wexp[:, :], ALU.mult))

            s_reg = dve.alloc_register("dve_slot")
            dve.wait_ge(pos_ready, 1)
            for u in range(2):
                dve.wait_ge(x2_st[u], 16 * (NT // 2 + 1))
                dve.wait_ge(xf_st[u], 16 * (NT // 2 + 1))

            def xgt_low(s):
                for b in range(2):
                    dve.wait_ge(xgt_hi, 2 * s + b + 1)
                    dve.scalar_tensor_tensor(xgt[1][:, 4 * b:4 * b + 4, :], ps[:, b, :].rearrange("p (k n) -> p k n", k=4), F_UP,
                                             xgt[0][:, 4 * b:4 * b + 4, :], ALU.mult, ALU.subtract).then_inc(xgt_done, 1)

            def hidt_low(s):
                dve.wait_ge(hidt_hi, s + 1)
                dve.tensor_tensor(hidt[1][:, :, :], ps[:, 6, :].rearrange("p (k n) -> p k n", k=KF), hidt[0][:, :, :],
                                  ALU.subtract).then_inc(hidt_done, 1)

            def y_out(s, slot):
                dve.wait_ge(g2_done, s + 1)
                dve.wait_ge(y_st, 16 * s + 16)
                dve.scalar_tensor_tensor(y_sb[:, :], banks(4, 2), 1.0 / (G_UP * W_UP), eb[slot][:, 2 * F:], ALU.mult, ALU.add).then_inc(y_ready, 1)

            def slot_dve(s, e, slot, other, convert, very_first=False):
                if not very_first:
                    hidt_low(s - 1)
                if convert:
                    for c in range(3 if very_first else EARLY):
                        econv_dve(dve, e + 1, 1 - slot, c, c % 4)
                dve.wait_ge(g1_done, s + 1)
                for b, g in enumerate((ga, gb)):
                    dve.scalar_tensor_tensor(g[:, :], ps[:, 2 + b, :], 1.0 / (F_UP * W_UP), eb[slot][:, b * F:(b + 1) * F],
                                             ALU.mult, ALU.add).then_inc(ab_done, 1)
                dve.wait_ge(silu_done, s + 1)
                dve.wait_ge(ab_done, 2 * s + 2)
                dve.scalar_tensor_tensor(hid[:, :], ga[:, :], G_UP, gb[:, :], ALU.mult, ALU.mult).then_inc(hid_ready, 1)
                xgt_low(s + 1)
                if not very_first:
                    y_out(s - 1, other)
                if convert:
                    for c in range(3 if very_first else EARLY, NC):
                        econv_dve(dve, e + 1, 1 - slot, c, c % 4)

            xgt_low(0)
            for c in range(KD, NC):
                econv_dve(dve, 0, 0, c, c % 4)

            def expert_dve(e, slot, turn, first=False, last=False):
                n = dve.value_load(toti[0:1, 1, ds(e, 1)], min_val=1, max_val=NT)
                wait_alone(dve, eb_ld[slot], 48 * turn)
                if first:
                    slot_dve(0, e, slot, None, True, very_first=True)
                    dve.reg_mov(s_reg, 1)
                else:
                    slot_dve(dve.snap(s_reg, min_val=1, max_val=SLOTS - 1), e, slot, 1 - slot, not last)
                    dve.reg_add(s_reg, s_reg, 1)
                with dve.If(n > 1):
                    with dve.Fori(1, n):
                        slot_dve(dve.snap(s_reg, min_val=1, max_val=SLOTS - 1), e, slot, slot, False)
                        dve.reg_add(s_reg, s_reg, 1)

            expert_dve(0, 0, 1, first=True)
            expert_dve(1, 1, 1)
            with dve.Fori(1, NE // 2 - 1) as j:
                expert_dve(2 * j, 0, j + 1)
                expert_dve(2 * j + 1, 1, j + 1)
            expert_dve(NE - 2, 0, NE // 2)
            expert_dve(NE - 1, 1, NE // 2, last=True)
            s_end = dve.snap(s_reg, min_val=1, max_val=SLOTS)
            hidt_low(s_end - 1)
            y_out(s_end - 1, 1)

            dve.wait_ge(x2e_ld, 16)
            for q in range(TOPK * NT):
                t, k = q // TOPK, q % TOPK
                rows = LAST if t == NT - 1 else P
                dve.wait_ge(yg_ld[q % RING], 16 * (q // RING + 1))
                if k:
                    dve.wait_ge(y_added, q)
                dve.scalar_tensor_tensor(x2e[0:rows, t, :], yg[q % RING][0:rows, :], wts[0:rows, k, t:t + 1], x2e[0:rows, t, :],
                                         ALU.mult, ALU.add).then_inc(y_added, 1)


def kernel(**inputs):
    import numpy as np
    import concourse.bacc as bacc
    from concourse.bass_utils import run_bass_kernel_spmd

    g = {k: np.asarray(v) for k, v in inputs.items()}
    n, d = g["x"].shape
    nt = -(-n // P)
    e = g["src"].shape[0]
    et = -(-e // P)
    eg = -(-et // P)
    rows = np.concatenate([g["dst"], np.full(eg * P * P - e, n - 1, g["dst"].dtype)])
    et += UNIT - 1
    src = np.concatenate([g["src"], np.full(et * P - e, -1, g["src"].dtype)])
    dst = np.concatenate([g["dst"], np.full(et * P - e, n - 1, g["dst"].dtype)])
    arrays = {
        "x": np.concatenate([g["x"], np.zeros((nt * P - n, d), g["x"].dtype)]),
        "src_t": src.reshape(et, P).T,
        "dst_t": dst.reshape(et, P).T,
        "dst_rows": rows.reshape(eg, P, P).transpose(1, 0, 2),
        "W": g["L0_gnn_W"],
        "a": g["L0_gnn_a"].reshape(2, d),
        "wqkv": g["L0_mix_w_qkv"].T,
        "wproj": g["L0_mix_w_proj"].T,
        "bproj": g["L0_mix_b_proj"].reshape(1, d),
        "ln_w": g["L0_ffn_ln_w"].reshape(1, d),
        "Wg": g["L0_ffn_Wg"],
        "bg": g["L0_ffn_bg"].reshape(1, -1),
        "W1a": g["L0_ffn_W1a"], "b1a": g["L0_ffn_b1a"], "W1b": g["L0_ffn_W1b"], "b1b": g["L0_ffn_b1b"],
        "W2": g["L0_ffn_W2"], "b2": g["L0_ffn_b2"],
    }
    nc = bacc.Bacc("TRN2", target_bir_lowering=False, num_devices=1)
    feed, args = {}, []
    for name, array in arrays.items():
        array = np.ascontiguousarray(array)
        feed[f"in_{name}"] = array
        args.append(nc.dram_tensor(f"in_{name}", array.shape, mybir.dt.from_np(array.dtype), kind="ExternalInput").ap())
    args.append(nc.dram_tensor("out_0", (n, d), F32, kind="ExternalOutput").ap())
    build(nc, *args)
    result = run_bass_kernel_spmd(nc, [feed], core_ids=[0])
    return result.results[0]["out_0"]
```
